# Optimizing a Trainium2 kernel written in Bass

```python
import numpy as np
import jax
import jax.numpy as jnp

def _softmax(x, axis=-1):
    return jax.nn.softmax(x, axis=axis)

def _gelu(x):
    return jax.nn.gelu(x, approximate=True)

def _silu(x):
    return jax.nn.silu(x)

def _sigmoid(x):
    return jax.nn.sigmoid(x)

def _layernorm(x, axis=-1, eps=1e-05):
    m = jnp.mean(x, axis=axis, keepdims=True)
    v = jnp.var(x, axis=axis, keepdims=True)
    return (x - m) / jnp.sqrt(v + eps)

def _scatter_add(tgt, idx, src, axis=0):
    return tgt.at[idx].add(src)

def _segment_sum(src, seg, n):
    return jax.ops.segment_sum(src, seg, n)
kernel_name = 'mk_gnn_preln_d1_gnn_r8_da88e5'

def setup_inputs(seed: int=0):
    np.random.seed(seed)
    _w = jnp.asarray

    def _rec_inputs():
        import jax
        import jax.numpy as jnp
        _gk = jax.random.key(seed)
        x = -0.000202 + 1 * jax.random.normal(jax.random.fold_in(_gk, 1), (12500, 128), jnp.float32)
        _s = jax.random.randint(jax.random.fold_in(_gk, 2), (200000,), 0, 12500, jnp.int32)
        _d = jax.random.randint(jax.random.fold_in(_gk, 3), (200000,), 0, 12500, jnp.int32)
        _loop = jnp.arange(12500, dtype=jnp.int32)
        src = jnp.concatenate([_s, _d, _loop])
        dst = jnp.concatenate([_d, _s, _loop])
        _o = jnp.argsort(dst, stable=True)
        src = src[_o]
        dst = dst[_o]
        edge_attr_64 = -5.3897e-05 + 0.999841 * jax.random.normal(jax.random.fold_in(_gk, 11), (412500, 64), jnp.float32)
        return (x, src, dst, edge_attr_64)
    x, src, dst, edge_attr_64 = _rec_inputs()

    def _L0_gnn_setup():
        import jax, jax.numpy as jnp
        import numpy as np
        N, E, D, DE, H = (6250, 50000, 128, 64, 8)
        EPS = 1e-05
        SLOPE = 0.2
        key = jax.random.key(seed)
        ks = jax.random.split(key, 16)

        def lin(k, fan_in, fan_out):
            return (jax.random.normal(k, (fan_in, fan_out), jnp.float32) / np.sqrt(fan_in)).astype(jnp.float32)
        return {'node_features': jax.random.normal(ks[0], (N, D), jnp.float32), 'edge_features': jax.random.normal(ks[1], (E, DE), jnp.float32), 'Wn': lin(ks[2], D, D), 'bn': jnp.zeros((D,), jnp.float32), 'Wq': lin(ks[3], D, D), 'bq': jnp.zeros((D,), jnp.float32), 'Wk': lin(ks[4], D, D), 'bk': jnp.zeros((D,), jnp.float32), 'Wv': lin(ks[5], D, D), 'bv': jnp.zeros((D,), jnp.float32), 'We': lin(ks[6], DE, D), 'be': jnp.zeros((D,), jnp.float32), 'A1': lin(ks[7], 3 * D, D), 'b1': jnp.zeros((D,), jnp.float32), 'A2': lin(ks[8], D, H), 'b2': jnp.zeros((H,), jnp.float32), 'gamma': jnp.ones((D,), jnp.float32), 'beta': jnp.zeros((D,), jnp.float32), 'edge_index': jax.random.randint(ks[9], (2, E), 0, N, dtype=jnp.int32)}
    _L0_gnn_all = _L0_gnn_setup()
    _L0_gnn_in = {k: v for k, v in _L0_gnn_all.items() if k in ('Wn', 'bn', 'Wq', 'bq', 'Wk', 'bk', 'Wv', 'bv', 'We', 'be', 'A1', 'b1', 'A2', 'b2', 'gamma', 'beta')}
    del _L0_gnn_all
    return {'x': x, 'src': src, 'dst': dst, 'edge_attr_64': edge_attr_64, 'L0_gnn_Wn': _L0_gnn_in['Wn'], 'L0_gnn_bn': _L0_gnn_in['bn'], 'L0_gnn_Wq': _L0_gnn_in['Wq'], 'L0_gnn_bq': _L0_gnn_in['bq'], 'L0_gnn_Wk': _L0_gnn_in['Wk'], 'L0_gnn_bk': _L0_gnn_in['bk'], 'L0_gnn_Wv': _L0_gnn_in['Wv'], 'L0_gnn_bv': _L0_gnn_in['bv'], 'L0_gnn_We': _L0_gnn_in['We'], 'L0_gnn_be': _L0_gnn_in['be'], 'L0_gnn_A1': _L0_gnn_in['A1'], 'L0_gnn_b1': _L0_gnn_in['b1'], 'L0_gnn_A2': _L0_gnn_in['A2'], 'L0_gnn_b2': _L0_gnn_in['b2'], 'L0_gnn_gamma': _L0_gnn_in['gamma'], 'L0_gnn_beta': _L0_gnn_in['beta']}

def reference(x, src, dst, edge_attr_64, L0_gnn_Wn, L0_gnn_bn, L0_gnn_Wq, L0_gnn_bq, L0_gnn_Wk, L0_gnn_bk, L0_gnn_Wv, L0_gnn_bv, L0_gnn_We, L0_gnn_be, L0_gnn_A1, L0_gnn_b1, L0_gnn_A2, L0_gnn_b2, L0_gnn_gamma, L0_gnn_beta):
    import jax
    import jax.numpy as jnp

    def _L0_gnn_ref(node_features, edge_features, Wn, bn, Wq, bq, Wk, bk, Wv, bv, We, be, A1, b1, A2, b2, gamma, beta, edge_index):
        import jax, jax.numpy as jnp
        import numpy as np
        N, E, D, DE, H = (6250, 50000, 128, 64, 8)
        EPS = 1e-05
        SLOPE = 0.2
        num_nodes = node_features.shape[0]
        h = node_features @ Wn + bn
        q = node_features @ Wq + bq
        k = node_features @ Wk + bk
        v = node_features @ Wv + bv
        eh = edge_features @ We + be
        src, tgt = (edge_index[0], edge_index[1])
        attn_in = jnp.concatenate([q[src], k[tgt], eh], axis=-1)
        hmid = jax.nn.leaky_relu(attn_in @ A1 + b1, SLOPE)
        scores = jax.nn.leaky_relu(hmid @ A2 + b2, SLOPE)
        w = jax.nn.softmax(scores.mean(axis=-1), axis=0)
        out = jax.ops.segment_sum(w[:, None] * v[tgt], src, num_segments=num_nodes)
        y = h + out
        mu = y.mean(axis=-1, keepdims=True)
        var = y.var(axis=-1, keepdims=True)
        return gamma * (y - mu) / jnp.sqrt(var + EPS) + beta
    edge_index = jnp.stack([src, dst])
    h = jnp.maximum(_layernorm(x, axis=-1), 0.0)
    x = x + _L0_gnn_ref(h, edge_attr_64, L0_gnn_Wn, L0_gnn_bn, L0_gnn_Wq, L0_gnn_bq, L0_gnn_Wk, L0_gnn_bk, L0_gnn_Wv, L0_gnn_bv, L0_gnn_We, L0_gnn_be, L0_gnn_A1, L0_gnn_b1, L0_gnn_A2, L0_gnn_b2, L0_gnn_gamma, L0_gnn_beta, edge_index)
    return x

_drawn_inputs = setup_inputs


def setup_inputs(seed=0):
    import zlib

    import numpy as np

    out = dict(_drawn_inputs(seed))
    spreads = {'L0_gnn_bn': (0.0, 0.1),
     'L0_gnn_bq': (0.0, 0.8),
     'L0_gnn_bk': (0.0, 0.8),
     'L0_gnn_bv': (0.0, 2.0),
     'L0_gnn_be': (0.0, 0.8),
     'L0_gnn_b1': (0.0, 0.8),
     'L0_gnn_b2': (0.0, 0.8),
     'L0_gnn_gamma': (1.0, 0.2),
     'L0_gnn_beta': (0.0, 0.1)}
    factors = {'edge_attr_64': 48.162,
     'L0_gnn_Wq': 54.797,
     'L0_gnn_Wk': 8.0,
     'L0_gnn_Wv': 64.0,
     'L0_gnn_We': 55.587,
     'L0_gnn_A1': 55.174,
     'L0_gnn_A2': 55.423}
    for name, (base, spread) in spreads.items():
        noise = np.random.default_rng([zlib.crc32(name.encode()), seed]).standard_normal(out[name].shape)
        drawn = base * np.exp(spread * noise) if base else spread * noise
        out[name] = jnp.asarray(drawn.astype(out[name].dtype))
    for name, factor in factors.items():
        out[name] = (out[name] * factor).astype(out[name].dtype)
    return out
```

```python
from contextlib import ExitStack

import concourse.bass as bass
from concourse import mybir

P = 128
PER = 8
GE = P * PER
UNROLL = 4
COPIES = 4
HALF = PER // 2
EPS = 1e-5
SLOPE = 0.2

ALU = mybir.AluOpType
ACT = mybir.ActivationFunctionType
F32 = mybir.dt.float32
BF16 = mybir.dt.bfloat16
I32 = mybir.dt.int32
AX_X = mybir.AxisListType.X
RMAX = bass.bass_isa.ReduceOp.max
RADD = bass.bass_isa.ReduceOp.add


def run_steps(eng, first, loop_from, loop_to, last, step):
    assert (loop_to + 1 - loop_from) % UNROLL == 0
    for s in range(first, loop_from):
        step(s, s % UNROLL)
    with eng.Fori(0, (loop_to + 1 - loop_from) // UNROLL) as i:
        for k in range(UNROLL):
            step(i * UNROLL + (loop_from + k), (loop_from + k) % UNROLL)
    for s in range(loop_to + 1, last + 1):
        step(s, s % UNROLL)


def known(s):
    return isinstance(s, int)


def at_least(s, n):
    return (not known(s)) or s >= n


def count(s, u, unit, ahead=0):
    g, v = s + ahead, (u + ahead) % UNROLL
    if known(s):
        return unit * (g // UNROLL + 1)
    return (g - v) * (unit // UNROLL) + unit


def gnn_layer(nc, x, src, dst, edge, Wn, bn, Wq, bq, Wk, bk, Wv, bv, We, be, A1, b1, A2, b2,
              gamma, beta, out):
    N, D = x.shape
    E, DE = edge.shape
    H = A2.shape[1]
    assert D == P and DE == P // 2
    FULL = E // GE
    LAST = FULL
    NG = FULL + 1
    TAIL0 = E - GE
    AGAIN = FULL * GE - TAIL0
    TR = N // P
    NREM = N - TR * P
    NT = TR + 1
    ROWS = -(-(N + P) // P) * P
    CH = -(-NG // P)
    assert E % GE and N % P

    q_tab = nc.dram_tensor("q_tab", [N, D], F32).ap()
    k_tab = nc.dram_tensor("k_tab", [N, D], F32).ap()
    v_tab = nc.dram_tensor("v_tab", [N, D], F32).ap()
    acc = [nc.dram_tensor(f"acc{r}", [ROWS, D], F32).ap() for r in range(COPIES)]

    def nodes_of(table, t, n, w=D):
        if known(t) and t == TR:
            return table[TR * P:N, :]
        return table[0:TR * P, :].rearrange("(p t) f -> p t f", t=TR)[:, bass.ds(t, n), :]

    with ExitStack() as ctx:
        def sb(name, shape, dt=F32):
            return ctx.enter_context(nc.sbuf_tensor(name, shape, dt))

        def sems(*names):
            return [ctx.enter_context(nc.semaphore(n)) for n in names]

        passed, = sems("passed")

        eps = sb("eps", [P, 1])
        ident = sb("ident", [P, P])
        ident_b = sb("ident_b", [P, P], BF16)
        earlier = sb("earlier", [P, P])
        part_i = sb("part_i", [P, 2], I32)
        part = sb("part", [P, 2])
        tail_mask = sb("tail_mask", [P, PER])
        x_sb = sb("x_sb", [P, NT, D])
        h_sb = sb("h_sb", [P, NT, D])
        w2 = sb("w2", [P, D])
        a2 = sb("a2", [P, H])
        b2_rep = sb("b2_rep", [P, PER, H])
        gamma_b = sb("gamma_b", [P, D])
        beta_b = sb("beta_b", [P, D])
        base_f = sb("base_f", [P, CH * P])
        base_i = sb("base_i", [P, CH * P], I32)
        local_i = sb("local_i", [P, 1], I32)
        score = sb("score", [P, NG * PER])
        weight = sb("weight", [P, NG * PER])

        NB = 4
        NSTEP = TR // NB
        assert TR % NB == 1
        with ExitStack() as st:
            def tmp(name, shape, dt=F32):
                return st.enter_context(nc.sbuf_tensor(name, shape, dt))

            def psum(name, shape):
                return st.enter_context(nc.psum_tensor(name, shape, F32))

            def sem(name):
                return st.enter_context(nc.semaphore(name))

            ZW = ROWS * D // P // 4
            zeros = tmp("zeros", [P, ZW])
            wm = tmp("wm", [P, 4 * D])
            bias = tmp("bias", [P, 4 * D])
            wq = tmp("wq", [P, D])
            wk = tmp("wk", [P, D])
            we = tmp("we", [DE, D])
            a1 = tmp("a1", [P, 3, D])
            bcol = tmp("bcol", [P, 3])
            b2_b = tmp("b2_b", [P, H])
            wqT = tmp("wqT", [P, D])
            wkT = tmp("wkT", [P, D])
            weT = tmp("weT", [P, 2, DE])
            stats = tmp("stats", [P, NT, 6])
            mv = tmp("mv", [P, NT, 2])
            std = tmp("std", [P, NT])
            rstd = tmp("rstd", [P, NT])
            xn = tmp("xn", [P, 2, NB, D])
            hT = tmp("hT", [P, 2, NB * P])
            tabs = tmp("tabs", [P, 2, 3, NB, D])
            dgroup = tmp("dgroup", [P, CH, GE], I32)
            dmin = tmp("dmin", [P, CH])
            dmax = tmp("dmax", [P, CH])
            dspan = tmp("dspan", [P, CH])
            span_row = tmp("span_row", [P, CH * P])
            span = tmp("span", [P, 1])
            ps_t = psum("ps_t", [P, 2, 512])
            ps_m = psum("ps_m", [P, NB, 512])
            ps_w = psum("ps_w", [P, 2, 512])

            made = sem("made")
            w_in = sem("w_in")
            x_in = sem("x_in")
            d_in = sem("d_in")
            zeroed = sem("zeroed")
            setup = sem("setup")
            w_turned = sem("w_turned")
            w_copied = sem("w_copied")
            w_made = sem("w_made")
            ready = sem("ready")
            stat_chain = sem("stat_chain")
            std_ready = sem("std_ready")
            xn_ready = sem("xn_ready")
            turned = sem("turned")
            hT_ready = sem("hT_ready")
            m_ready = sem("m_ready")
            tab_ready = sem("tab_ready")
            stored = [sem("stored0"), sem("stored1")]
            span_chain = sem("span_chain")
            span_turned = sem("span_turned")

            N_MADE = 12
            LOADS = 18

            with nc.Block() as block:
                @block.gpsimd
                def _(pool):
                    nc.gpsimd.memset(zeros[:], 0.0).then_inc(made, 1)
                    nc.gpsimd.memset(x_sb[:, TR, :], 0.0).then_inc(made, 1)
                    nc.gpsimd.memset(dgroup[:, CH - 1, :], 0).then_inc(made, 1)
                    nc.gpsimd.memset(eps[:], EPS).then_inc(made, 1)
                    nc.gpsimd.memset(ident[:], 0.0).then_inc(made, 1)
                    nc.gpsimd.memset(earlier[:], 1.0).then_inc(made, 1)
                    nc.gpsimd.memset(tail_mask[:], 1.0).then_inc(made, 1)
                    pool.wait_ge(made, 7)
                    nc.gpsimd.affine_select(out=ident[:], in_=ident[:], compare_op=ALU.not_equal, fill=1.0,
                                            base=0, pattern=[[-1, P]], channel_multiplier=1).then_inc(made, 1)
                    nc.gpsimd.affine_select(out=earlier[:], in_=earlier[:], compare_op=ALU.is_gt, fill=0.0,
                                            base=0, pattern=[[-1, P]], channel_multiplier=1).then_inc(made, 1)
                    nc.gpsimd.affine_select(out=tail_mask[:], in_=tail_mask[:], compare_op=ALU.is_ge, fill=0.0,
                                            base=-AGAIN, pattern=[[1, PER]], channel_multiplier=PER).then_inc(made, 1)
                    nc.gpsimd.iota(part_i[:, 0:1], [[0, 1]], base=0, channel_multiplier=1).then_inc(made, 1)
                    nc.gpsimd.iota(part_i[:, 1:2], [[0, 1]], base=N, channel_multiplier=1).then_inc(made, 1)

                @block.sync
                def _(sp):
                    row = lambda v: v.rearrange("(a d) -> a d", a=1).to_broadcast([P, v.shape[0]])
                    col = lambda v: v.rearrange("(d a) -> d a", a=1)
                    loads = [
                        (wm[:, 0:D], Wn), (wm[:, 3 * D:4 * D], Wv), (wq[:], Wq), (wk[:], Wk), (we[:], We),
                        (a1[:], A1.rearrange("(c p) f -> p c f", p=P)), (a2[:], A2),
                        (bcol[:, 0:1], col(bq)), (bcol[:, 1:2], col(bk)), (bcol[:, 2:3], col(be)),
                        (bias[:, 0:D], row(bn)), (bias[:, 2 * D:3 * D], row(b1)), (bias[:, 3 * D:4 * D], row(bv)),
                        (b2_b[:], row(b2)), (gamma_b[:], row(gamma)), (beta_b[:], row(beta)),
                    ]
                    assert len(loads) == LOADS - 2
                    for d, s in loads:
                        sp.dma_start(d, s).then_inc(w_in, 16)
                    sp.dma_start(x_sb[:, 0:TR, :], nodes_of(x, 0, TR)).then_inc(x_in, 16)
                    sp.wait_ge(made, 3)
                    sp.dma_start(x_sb[0:NREM, TR, :], nodes_of(x, TR, 1)).then_inc(x_in, 16)
                    for c in range(CH - 1):
                        sp.dma_start(dgroup[:, c, :], dst[c * P * GE:(c + 1) * P * GE].rearrange("(g e) -> g e", g=P)
                                     ).then_inc(d_in, 16)
                    rest = FULL - (CH - 1) * P
                    sp.dma_start(dgroup[0:rest, CH - 1, :],
                                 dst[(CH - 1) * P * GE:FULL * GE].rearrange("(g e) -> g e", g=rest)).then_inc(d_in, 16)
                    sp.dma_start(dgroup[rest:rest + 1, CH - 1, :],
                                 dst[TAIL0:E].rearrange("(g e) -> g e", g=1)).then_inc(d_in, 16)
                    for r in range(COPIES):
                        for c in range(4):
                            sp.dma_start(acc[r].rearrange("(p a) f -> p (a f)", p=P)[:, c * ZW:(c + 1) * ZW],
                                         zeros[:]).then_inc(zeroed, 16)

                    def store(s, u, n=NB, t=None):
                        sp.wait_ge(tab_ready, (s + 1) * 2 * NB if n == NB else 2 * NB * NSTEP + 4)
                        for i, table in enumerate((q_tab, k_tab, v_tab)):
                            sp.dma_start(nodes_of(table, s * NB, n) if t is None else nodes_of(table, t, 1),
                                         tabs[:, u, i, 0:n, :] if t is None else tabs[0:NREM, u, i, 1, :]
                                         ).then_inc(stored[u], 16)

                    with sp.Fori(0, NSTEP // 2) as i:
                        for u in range(2):
                            store(i * 2 + u, u)
                    store(NSTEP, NSTEP % 2, 1)
                    store(NSTEP, NSTEP % 2, 1, TR)
                    sp.wait_ge(stored[0], 48 * (NSTEP // 2) + 96)
                    sp.wait_ge(stored[1], 48 * (NSTEP // 2))
                    sp.wait_ge(zeroed, 64 * COPIES)

                def node_steps(eng, step):
                    step(0, 0)
                    step(1, 1)
                    with eng.Fori(1, NSTEP // 2) as i:
                        for u in range(2):
                            step(i * 2 + u, u)
                    step(NSTEP, 0)

                def tiles(s):
                    return 2 if known(s) and s == NSTEP else NB

                @block.tensor
                def _(pe):
                    pe.wait_ge(made, N_MADE)
                    pe.wait_ge(w_in, 16 * (LOADS - 2))
                    pe.transpose(ps_w[:, 0, 0:P], wq[:], ident[:])
                    pe.transpose(ps_w[:, 0, P:2 * P], wk[:], ident[:])
                    pe.transpose(ps_w[:, 0, 2 * P:2 * P + DE], we[:], ident[0:DE, 0:DE]).then_inc(w_turned, 1)
                    pe.wait_ge(w_copied, 4)
                    pe.matmul(ps_w[:, 1, 0:P], wqT[:], a1[:, 0, :], start=True, stop=True)
                    pe.matmul(ps_w[:, 1, P:2 * P], wkT[:], a1[:, 1, :], start=True, stop=True)
                    pe.matmul(ps_w[:, 1, 2 * P:3 * P], weT[:].rearrange("p a k -> p (a k)"), a1[:, 2, :],
                              start=True, stop=True)
                    pe.matmul(ps_w[:, 0, 0:P], bcol[:, 0:1].to_broadcast([P, P]), a1[:, 0, :], start=True, stop=True)
                    pe.matmul(ps_w[:, 0, P:2 * P], bcol[:, 1:2].to_broadcast([P, P]), a1[:, 1, :], start=True, stop=False)
                    pe.matmul(ps_w[:, 0, P:2 * P], bcol[:, 2:3].to_broadcast([P, P]), a1[:, 2, :], start=False,
                              stop=True).then_inc(w_made, 1)
                    pe.wait_ge(ready, 6 + PER)

                    def turn(s, u):
                        pe.wait_ge(xn_ready, (s + 1) * NB if tiles(s) == NB else NB * NSTEP + 2)
                        if at_least(s, 2):
                            pe.wait_ge(hT_ready, s - 1)
                        for k in range(tiles(s)):
                            last = pe.transpose(ps_t[:, u, k * P:(k + 1) * P], xn[:, u, k, :], ident[:])
                        last.then_inc(turned, 1)

                    def project(s, u):
                        pe.wait_ge(hT_ready, s + 1)
                        for k in range(tiles(s)):
                            if at_least(s, 1):
                                pe.wait_ge(tab_ready, s * (2 * NB) - 2 * (NB - 1 - k))
                            pe.matmul(ps_m[:, k, :], hT[:, u, k * P:(k + 1) * P], wm[:], start=True,
                                      stop=True).then_inc(m_ready, 1)

                    def step(s, u):
                        turn(s, u)
                        project(s, u)

                    node_steps(pe, step)
                    pe.wait_ge(span_chain, 4)
                    for c in range(CH):
                        pe.matmul(ps_w[:, 0, c * P:(c + 1) * P], dmin[:, c:c + 1].to_broadcast([P, P]), ident[:],
                                  start=True, stop=True)
                        last = pe.matmul(ps_w[:, 1, c * P:(c + 1) * P], dspan[:, c:c + 1].to_broadcast([P, P]), ident[:],
                                         start=True, stop=True)
                    last.then_inc(span_turned, 1)

                @block.scalar
                def _(act):
                    act.wait_ge(stat_chain, 2 * NT)
                    nc.scalar.activation(std[:], mv[:, :, 1], ACT.Sqrt, bias=eps[:, 0:1]).then_inc(std_ready, 1)

                    def step(s, u):
                        act.wait_ge(turned, s + 1)
                        if at_least(s, 2):
                            act.wait_ge(m_ready, (s - 1) * NB)
                        w = tiles(s) * P
                        nc.scalar.activation(hT[:, u, 0:w], ps_t[:, u, 0:w], ACT.Relu).then_inc(hT_ready, 1)

                    node_steps(act, step)

                @block.vector
                def _(dve):
                    dve.wait_ge(w_turned, 1)
                    nc.vector.tensor_copy(wqT[:], ps_w[:, 0, 0:P]).then_inc(w_copied, 1)
                    nc.vector.tensor_copy(wkT[:], ps_w[:, 0, P:2 * P]).then_inc(w_copied, 1)
                    nc.vector.tensor_copy(weT[:, 0, :], ps_w[:, 0, 2 * P:2 * P + DE]).then_inc(w_copied, 1)
                    nc.vector.tensor_copy(weT[:, 1, :], ps_w[:, 0, 2 * P:2 * P + DE]).then_inc(w_copied, 1)
                    dve.wait_ge(w_made, 1)
                    nc.vector.tensor_copy(wm[:, D:3 * D], ps_w[:, 1, 0:2 * D]).then_inc(ready, 1)
                    nc.vector.tensor_copy(w2[:], ps_w[:, 1, 2 * D:3 * D]).then_inc(ready, 1)
                    nc.vector.tensor_copy(bias[:, D:2 * D], ps_w[:, 0, 0:D]).then_inc(ready, 1)
                    nc.vector.tensor_tensor(bias[:, 2 * D:3 * D], bias[:, 2 * D:3 * D], ps_w[:, 0, D:2 * D],
                                            ALU.add).then_inc(ready, 1)
                    for j in range(PER):
                        nc.vector.tensor_copy(b2_rep[:, j, :], b2_b[:]).then_inc(ready, 1)
                    nc.vector.tensor_copy(part[:], part_i[:]).then_inc(ready, 1)
                    nc.vector.tensor_copy(ident_b[:], ident[:]).then_inc(ready, 1)
                    dve.wait_ge(x_in, 32)
                    with dve.Fori(0, NT) as t:
                        nc.vector.bn_stats(stats[:, bass.ds(t, 1), :].rearrange("p a k -> p (a k)"),
                                           x_sb[:, bass.ds(t, 1), :].rearrange("p a k -> p (a k)")).then_inc(stat_chain, 1)
                    dve.wait_ge(stat_chain, NT)
                    for t in range(NT):
                        nc.vector.bn_aggr(mv[:, t, :], stats[:, t, :]).then_inc(stat_chain, 1)
                    dve.wait_ge(std_ready, 1)
                    nc.vector.reciprocal(rstd[:], std[:]).then_inc(ready, 1)
                    dve.wait_ge(ready, 7 + PER)

                    def normal(s, u):
                        if at_least(s, 2):
                            dve.wait_ge(turned, s - 1)
                        for k in range(tiles(s)):
                            t = s * NB + k
                            nc.vector.tensor_scalar(xn[:, u, k, :], x_sb[:, bass.ds(t, 1), :].rearrange("p a k -> p (a k)"),
                                                    mv[:, bass.ds(t, 1), 0:1].rearrange("p a k -> p (a k)"),
                                                    rstd[:, bass.ds(t, 1)], ALU.subtract, ALU.mult).then_inc(xn_ready, 1)

                    def add_bias(s, u):
                        if at_least(s, 2):
                            dve.wait_ge(stored[u], (s - u) * 24)
                        for k in range(tiles(s)):
                            dve.wait_ge(m_ready, s * NB + (k + 1))
                            nc.vector.tensor_tensor(h_sb[:, bass.ds(s * NB + k, 1), :].rearrange("p a k -> p (a k)"),
                                                    ps_m[:, k, 0:D], bias[:, 0:D], ALU.add).then_inc(tab_ready, 1)
                            nc.vector.tensor_tensor(tabs[:, u, :, k, :], ps_m[:, k, D:4 * D].rearrange("p (a f) -> p a f", a=3),
                                                    bias[:, D:4 * D].rearrange("p (a f) -> p a f", a=3),
                                                    ALU.add).then_inc(tab_ready, 1)

                    def step(s, u):
                        if known(s) and s == 0:
                            normal(0, 0)
                        if not (known(s) and s == NSTEP):
                            normal(s + 1, 1 - u)
                        add_bias(s, u)

                    step(0, 0)
                    step(1, 1)
                    with dve.Fori(1, NSTEP // 2 - 1) as i:
                        for u in range(2):
                            step(i * 2 + u, u)
                    step(NSTEP - 2, 0)
                    step(NSTEP - 1, 1)
                    step(NSTEP, 0)
                    dve.wait_ge(d_in, 16 * (CH + 1))
                    nc.vector.tensor_reduce(dmin[:], dgroup[:], AX_X, ALU.min).then_inc(span_chain, 1)
                    nc.vector.tensor_reduce(dmax[:], dgroup[:], AX_X, ALU.max).then_inc(span_chain, 1)
                    dve.wait_ge(span_chain, 2)
                    nc.vector.tensor_scalar(dmin[:], dmin[:], float(N - P), None, ALU.min).then_inc(span_chain, 1)
                    dve.wait_ge(span_chain, 3)
                    nc.vector.tensor_tensor(dspan[:], dmax[:], dmin[:], ALU.subtract).then_inc(span_chain, 1)
                    dve.wait_ge(span_turned, 1)
                    nc.vector.tensor_copy(base_f[:], ps_w[:, 0, 0:CH * P]).then_inc(span_chain, 1)
                    nc.vector.tensor_copy(base_i[:], ps_w[:, 0, 0:CH * P]).then_inc(span_chain, 1)
                    nc.vector.tensor_reduce(span[:], ps_w[:, 1, 0:CH * P], AX_X, ALU.max).then_inc(span_chain, 1)
                    dve.wait_ge(span_chain, 7)
                    nc.vector.tensor_scalar(local_i[:], span[:], float(P - 1), None, ALU.is_le).then_inc(span_chain, 1)

        def group_edges(s):
            return TAIL0 if known(s) and s == LAST else s * GE

        L0, L1 = 3, 3 + UNROLL * ((NG - 1 - 3 - 1) // UNROLL) - 1
        LASTSTEP = NG

        def branches(eng, with_window, with_gather):
            flag = eng.value_load(local_i[0:1, 0:1], min_val=0, max_val=1)
            with eng.If(flag):
                with_window()
            with eng.Else():
                with_gather()

        def in_group(s, n):
            return (not known(s)) or 0 <= s + n < NG

        with ExitStack() as st:
            def tmp(name, shape, dt=F32):
                return st.enter_context(nc.sbuf_tensor(name, shape, dt))

            def psum(name, shape):
                return st.enter_context(nc.psum_tensor(name, shape, F32))

            def sem(name):
                return st.enter_context(nc.semaphore(name))

            edges = tmp("edges", [P, UNROLL, PER, DE])
            src_i = tmp("src_i", [P, UNROLL, PER], I32)
            dst_i = tmp("dst_i", [P, UNROLL, PER], I32)
            q_rows = tmp("q_rows", [P, UNROLL, PER, D])
            k_rows = tmp("k_rows", [P, UNROLL, PER, D])
            k_win = k_rows
            rel = tmp("rel", [P, 2, PER], BF16)
            onehot = tmp("onehot", [P, 2, PER, P])
            edgeT = tmp("edgeT", [P, 2, HALF, P])
            low = tmp("low", [P, 2, PER, P])
            mid = tmp("mid", [P, 2, PER, P])
            head = tmp("head", [P, 2, PER, H])
            head2 = tmp("head2", [P, 2, PER, H])
            ps_rel = psum("ps_rel", [P, PER, P])
            ps_z = psum("ps_z", [P, 2, PER, P])
            ps_e = psum("ps_e", [P, HALF, P])
            ps_s = psum("ps_s", [P, 2, PER, H])

            edges_in = [sem(f"edges_in{u}") for u in range(UNROLL)]
            src_in = [sem(f"src_in{u}") for u in range(UNROLL)]
            dst_in = [sem(f"dst_in{u}") for u in range(UNROLL)]
            q_in = [sem(f"q_in{u}") for u in range(UNROLL)]
            k_in = [sem(f"k_in{u}") for u in range(UNROLL)]
            edge_turned = sem("edge_turned")
            edgeT_ready = sem("edgeT_ready")
            rel_ready = sem("rel_ready")
            rel_spread = sem("rel_spread")
            onehot_ready = sem("onehot_ready")
            z_ready = sem("z_ready")
            low_ready = sem("low_ready")
            mid_ready = sem("mid_ready")
            s_ready = sem("s_ready")
            score_chain = sem("score_chain")

            def tile_at(b, k):
                return 2 * k + b

            with nc.Block() as block:
                @block.sync
                def _(sp):
                    def load(s, u, window):
                        e0 = group_edges(s)
                        if at_least(s, UNROLL):
                            sp.wait_ge(edge_turned, s - (UNROLL - 1))
                            sp.sem_inc(passed, 1)
                        sp.dma_start(edges[:, u, :, :], edge[bass.ds(e0, GE), :].rearrange("(p j) f -> p j f", p=P)
                                     ).then_inc(edges_in[u], 16)
                        if at_least(s, UNROLL):
                            sp.wait_ge(q_in[u], count(s, u, 16 * PER, -UNROLL))
                            sp.sem_inc(passed, 1)
                        sp.dma_start(src_i[:, u, :], src[bass.ds(e0, GE)].rearrange("(p j) -> p j", p=P)
                                     ).then_inc(src_in[u], 16)
                        if at_least(s, UNROLL):
                            if window:
                                sp.wait_ge(rel_ready, s - (UNROLL - 1))
                            else:
                                sp.wait_ge(k_in[u], count(s, u, 16 * PER, -UNROLL))
                            sp.sem_inc(passed, 1)
                        sp.dma_start(dst_i[:, u, :], dst[bass.ds(e0, GE)].rearrange("(p j) -> p j", p=P)
                                     ).then_inc(dst_in[u], 16)
                        if window:
                            if at_least(s, UNROLL):
                                sp.wait_ge(z_ready, s * 2 - (2 * UNROLL - 2))
                            sp.sem_inc(passed, 1)
                            row = sp.value_load(base_i[0:1, bass.ds(s, 1)], min_val=0, max_val=N - P)
                            sp.dma_start(k_win[:, u, 0, :], k_tab[bass.ds(row, P), :]).then_inc(k_in[u], 16)

                    branches(sp, lambda: run_steps(sp, 0, UNROLL, UNROLL * (LAST // UNROLL) - 1, LAST, lambda s, u: load(s, u, True)),
                             lambda: run_steps(sp, 0, UNROLL, UNROLL * (LAST // UNROLL) - 1, LAST, lambda s, u: load(s, u, False)))

                @block.gpsimd
                def _(pool):
                    def gather(s, u, window):
                        pool.wait_ge(src_in[u], count(s, u, 16))
                        if at_least(s, UNROLL):
                            pool.wait_ge(z_ready, s * 2 - (2 * UNROLL - 2))
                        pool.sem_inc(passed, 1)
                        for j in range(PER):
                            pool.indirect_dma_start(q_rows[:, u, j, :], None, q_tab,
                                                    bass.IndirectOffsetOnAxis(src_i[:, u, j:j + 1], 0)
                                                    ).then_inc(q_in[u], 16)
                        if not window:
                            pool.wait_ge(dst_in[u], count(s, u, 16))
                            pool.sem_inc(passed, 1)
                            for j in range(PER):
                                pool.indirect_dma_start(k_rows[:, u, j, :], None, k_tab,
                                                        bass.IndirectOffsetOnAxis(dst_i[:, u, j:j + 1], 0)
                                                        ).then_inc(k_in[u], 16)

                    branches(pool, lambda: run_steps(pool, 0, UNROLL, UNROLL * (LAST // UNROLL) - 1, LAST, lambda s, u: gather(s, u, True)),
                             lambda: run_steps(pool, 0, UNROLL, UNROLL * (LAST // UNROLL) - 1, LAST, lambda s, u: gather(s, u, False)))

                @block.tensor
                def _(pe):
                    def turn(s, u):
                        pe.wait_ge(edges_in[u], count(s, u, 16))
                        if at_least(s, 1):
                            pe.wait_ge(edgeT_ready, s)
                        for k in range(HALF):
                            last = pe.transpose(ps_e[:, k, :], edges[:, u, 2 * k:2 * k + 2, :].rearrange("p j f -> p (j f)"),
                                                ident[:])
                        last.then_inc(edge_turned, 1)

                    def spread(s, u):
                        pe.wait_ge(rel_ready, s + 1)
                        if at_least(s, 1):
                            pe.wait_ge(onehot_ready, s)
                        for b in range(2):
                            for k in range(HALF):
                                last = pe.matmul(ps_rel[:, HALF * b + k, :],
                                                 rel[:, u % 2, tile_at(b, k):tile_at(b, k) + 1].to_broadcast([P, P]),
                                                 ident_b[:], start=True, stop=True)
                        last.then_inc(rel_spread, 1)

                    def make_z(s, u, window):
                        pe.wait_ge(edgeT_ready, s + 1)
                        pe.wait_ge(k_in[u], count(s, u, 16 if window else 16 * PER))
                        if window:
                            pe.wait_ge(onehot_ready, s + 1)
                        if at_least(s, 2):
                            pe.wait_ge(mid_ready, s * 2 - 2)
                        for b in range(2):
                            bank = ps_z[:, u % 2, HALF * b:HALF * (b + 1), :]
                            lo = DE * b
                            pe.matmul(bank.rearrange("p k e -> p (k e)"), w2[lo:lo + DE, :],
                                      edgeT[lo:lo + DE, u % 2, :, :].rearrange("p k e -> p (k e)"),
                                      start=True, stop=False, skip_group_check=True)
                            if window:
                                pe.matmul(bank.rearrange("p k e -> p (k e)"), k_win[:, u, 0, :],
                                          onehot[:, u % 2, HALF * b:HALF * (b + 1), :].rearrange("p k e -> p (k e)"),
                                          start=False, stop=False, skip_group_check=True)
                            if b == 0:
                                pe.wait_ge(q_in[u], count(s, u, 16 * PER))
                            for k in range(HALF):
                                if not window:
                                    pe.matmul(ps_z[:, u % 2, HALF * b + k, :], k_rows[:, u, tile_at(b, k), :], ident[:],
                                              start=False, stop=False, skip_group_check=True)
                                last = pe.matmul(ps_z[:, u % 2, HALF * b + k, :], q_rows[:, u, tile_at(b, k), :], ident[:],
                                                 start=False, stop=(k == HALF - 1), skip_group_check=True)
                            last.then_inc(z_ready, 1)

                    def heads(s, u):
                        pe.wait_ge(mid_ready, s * 2 + 2)
                        if at_least(s, 1):
                            pe.wait_ge(score_chain, s * 3 - 2)
                        for b in range(2):
                            for k in range(HALF):
                                last = pe.matmul(ps_s[:, u % 2, tile_at(b, k), :], mid[:, u % 2, HALF * b + k, :], a2[:],
                                                 start=True, stop=True)
                        last.then_inc(s_ready, 1)

                    def step(s, u, window):
                        if in_group(s, 1):
                            turn(s + 1, (u + 1) % UNROLL)
                            if window:
                                spread(s + 1, (u + 1) % UNROLL)
                        if in_group(s, 0):
                            make_z(s, u, window)
                        if at_least(s, 1):
                            heads(s - 1, (u - 1) % UNROLL)

                    def path(window):
                        turn(0, 0)
                        if window:
                            spread(0, 0)
                        run_steps(pe, 0, L0, L1, LASTSTEP, lambda s, u: step(s, u, window))

                    branches(pe, lambda: path(True), lambda: path(False))

                @block.scalar
                def _(act):
                    def copy_edges(s, u):
                        act.wait_ge(edge_turned, s + 1)
                        if at_least(s, 2):
                            act.wait_ge(z_ready, s * 2 - 2)
                        nc.scalar.activation(edgeT[:, u % 2, :, :], ps_e[:], ACT.Copy).then_inc(edgeT_ready, 1)

                    def scale(s, u):
                        for b in range(2):
                            act.wait_ge(z_ready, s * 2 + (b + 1))
                            if at_least(s, 2):
                                act.wait_ge(mid_ready, s * 2 - (3 - b))
                            h0, h1 = HALF * b, HALF * (b + 1)
                            nc.scalar.activation(low[:, u % 2, h0:h1, :], ps_z[:, u % 2, h0:h1, :], ACT.Copy,
                                                 scale=SLOPE).then_inc(low_ready, 1)

                    def step(s, u):
                        if in_group(s, 1):
                            copy_edges(s + 1, (u + 1) % UNROLL)
                        if in_group(s, 0):
                            scale(s, u)

                    copy_edges(0, 0)
                    run_steps(act, 0, L0, L1, LAST, step)

                @block.vector
                def _(dve):
                    def relative(s, u):
                        dve.wait_ge(dst_in[u], count(s, u, 16))
                        if at_least(s, 2):
                            dve.wait_ge(rel_spread, s - 1)
                        nc.vector.tensor_tensor(rel[:, u % 2, :], dst_i[:, u, :], base_f[:, bass.ds(s, 1)].to_broadcast([P, PER]),
                                                ALU.subtract).then_inc(rel_ready, 1)

                    def one_hot(s, u):
                        dve.wait_ge(rel_spread, s + 1)
                        if at_least(s, 2):
                            dve.wait_ge(z_ready, s * 2 - 2)
                        nc.vector.tensor_scalar(onehot[:, u % 2, :, :], ps_rel[:], part[:, 0:1], None,
                                                ALU.is_equal).then_inc(onehot_ready, 1)

                    def leaky(s, u):
                        if at_least(s, 2):
                            dve.wait_ge(s_ready, s - 1)
                        for b in range(2):
                            dve.wait_ge(low_ready, s * 2 + (b + 1))
                            h0, h1 = HALF * b, HALF * (b + 1)
                            nc.vector.tensor_tensor(mid[:, u % 2, h0:h1, :], low[:, u % 2, h0:h1, :],
                                                    ps_z[:, u % 2, h0:h1, :], ALU.max).then_inc(mid_ready, 1)

                    def head_sum(s, u):
                        dve.wait_ge(s_ready, s + 1)
                        nc.vector.tensor_tensor(head[:, u % 2, :, :], ps_s[:, u % 2, :, :], b2_rep[:],
                                                ALU.add).then_inc(score_chain, 1)
                        dve.wait_ge(score_chain, s * 3 + 1)
                        nc.vector.scalar_tensor_tensor(head2[:, u % 2, :, :], head[:, u % 2, :, :], SLOPE,
                                                       head[:, u % 2, :, :], ALU.mult, ALU.max).then_inc(score_chain, 1)
                        dve.wait_ge(score_chain, s * 3 + 2)
                        nc.vector.tensor_reduce(score[:, bass.ds(s * PER, PER)], head2[:, u % 2, :, :], AX_X,
                                                ALU.add).then_inc(score_chain, 1)

                    def step(s, u, window):
                        if window:
                            if in_group(s, 2):
                                relative(s + 2, (u + 2) % UNROLL)
                            if in_group(s, 1):
                                one_hot(s + 1, (u + 1) % UNROLL)
                        if in_group(s, 0):
                            leaky(s, u)
                        if at_least(s, 1):
                            head_sum(s - 1, (u - 1) % UNROLL)

                    def path(window):
                        if window:
                            relative(0, 0)
                            relative(1, 1)
                            one_hot(0, 0)
                        run_steps(dve, 0, L0, L1, LASTSTEP, lambda s, u: step(s, u, window))

                    branches(dve, lambda: path(True), lambda: path(False))

        with ExitStack() as st:
            def tmp(name, shape, dt=F32):
                return st.enter_context(nc.sbuf_tensor(name, shape, dt))

            def sem(name):
                return st.enter_context(nc.semaphore(name))

            top = tmp("top", [P, 1])
            top_all = tmp("top_all", [P, 1])
            shift = tmp("shift", [P, 1])
            sums = tmp("sums", [P, 2])
            total = tmp("total", [P, 1])
            total_all = tmp("total_all", [P, 1])
            inv = tmp("inv", [P, 1])
            top_ready = sem("top_ready")
            top_spread = sem("top_spread")
            shifted = sem("shifted")
            exp_ready = sem("exp_ready")
            sum_chain = sem("sum_chain")
            sum_spread = sem("sum_spread")
            NF = FULL * PER

            with nc.Block() as block:
                @block.gpsimd
                def _(pool):
                    pool.wait_ge(top_ready, 1)
                    nc.gpsimd.partition_all_reduce(top_all[:], top[:], P, RMAX).then_inc(top_spread, 1)
                    pool.wait_ge(sum_chain, 3)
                    nc.gpsimd.partition_all_reduce(total_all[:], total[:], P, RADD).then_inc(sum_spread, 1)

                @block.scalar
                def _(act):
                    act.wait_ge(top_spread, 1)
                    nc.scalar.mul(shift[:], top_all[:], -1.0 / H).then_inc(shifted, 1)
                    act.wait_ge(shifted, 1)
                    nc.scalar.activation(weight[:, 0:NF], score[:, 0:NF], ACT.Exp, bias=shift[:, 0:1], scale=1.0 / H,
                                         accum_out=sums[:, 0:1]).then_inc(exp_ready, 1)
                    nc.scalar.activation(weight[:, NF:], score[:, NF:], ACT.Exp, bias=shift[:, 0:1],
                                         scale=1.0 / H).then_inc(exp_ready, 1)

                @block.vector
                def _(dve):
                    nc.vector.tensor_reduce(top[:], score[:], AX_X, ALU.max).then_inc(top_ready, 1)
                    dve.wait_ge(exp_ready, 2)
                    nc.vector.tensor_tensor(weight[:, NF:], weight[:, NF:], tail_mask[:], ALU.mult).then_inc(sum_chain, 1)
                    dve.wait_ge(sum_chain, 1)
                    nc.vector.tensor_reduce(sums[:, 1:2], weight[:, NF:], AX_X, ALU.add).then_inc(sum_chain, 1)
                    dve.wait_ge(sum_chain, 2)
                    nc.vector.tensor_tensor(total[:], sums[:, 0:1], sums[:, 1:2], ALU.add).then_inc(sum_chain, 1)
                    dve.wait_ge(sum_spread, 1)
                    nc.vector.reciprocal(inv[:], total_all[:]).then_inc(sum_chain, 1)
                    dve.wait_ge(sum_chain, 4)
                    nc.vector.tensor_scalar(weight[:], weight[:], inv[:, 0:1], None, ALU.mult).then_inc(sum_chain, 1)

        with ExitStack() as st:
            def tmp(name, shape, dt=F32):
                return st.enter_context(nc.sbuf_tensor(name, shape, dt))

            def psum(name, shape):
                return st.enter_context(nc.psum_tensor(name, shape, F32))

            def sem(name):
                return st.enter_context(nc.semaphore(name))

            src_j = tmp("src_j", [P, UNROLL, PER], I32)
            dst_j = tmp("dst_j", [P, UNROLL, PER], I32)
            src_f = tmp("src_f", [P, UNROLL, PER])
            w_now = tmp("w_now", [P, UNROLL, PER])
            rel_j = tmp("rel_j", [P, 2, PER], BF16)
            one_j = tmp("one_j", [P, 2, PER, P])
            v_rows = tmp("v_rows", [P, UNROLL, PER, D])
            v_win = tmp("v_win", [P, UNROLL, D])
            same_w = tmp("same_w", [P, 2, PER, P])
            same_b = tmp("same_b", [P, PER, P])
            before = tmp("before", [P, UNROLL, PER])
            dup = tmp("dup", [P, UNROLL, PER])
            move = tmp("move", [P, UNROLL, PER])
            row_i = tmp("row_i", [P, UNROLL, PER], I32)
            summed = tmp("summed", [P, UNROLL, PER, D])
            ps_r = psum("ps_r", [P, PER, P])
            ps_src = psum("ps_src", [P, PER, P])
            ps_v = psum("ps_v", [P, PER, P])
            ps_x = psum("ps_x", [P, PER, P])

            src_in = [sem(f"srcj_in{u}") for u in range(UNROLL)]
            dst_in = [sem(f"dstj_in{u}") for u in range(UNROLL)]
            v_in = [sem(f"v_in{u}") for u in range(UNROLL)]
            prep = sem("prep")
            rel_ready = sem("relj_ready")
            spread_done = sem("spread_done")
            rel_spread = sem("relj_spread")
            one_ready = sem("onej_ready")
            same_ready = sem("same_ready")
            row_chain = sem("row_chain")
            v_made = sem("v_made")
            v_copied = sem("v_copied")
            x_made = sem("x_made")
            x_copied = sem("x_copied")
            added = [sem(f"added{r}") for r in range(COPIES)]
            AC = PER // COPIES
            J0, J1 = L0, L1
            JLAST = NG

            with nc.Block() as block:
                @block.sync
                def _(sp):
                    def load(s, u, window):
                        e0 = group_edges(s)
                        if at_least(s, UNROLL):
                            sp.wait_ge(prep, s * 2 - (2 * UNROLL - 2))
                            sp.sem_inc(passed, 1)
                        sp.dma_start(src_j[:, u, :], src[bass.ds(e0, GE)].rearrange("(p j) -> p j", p=P)
                                     ).then_inc(src_in[u], 16)
                        if at_least(s, UNROLL):
                            if window:
                                sp.wait_ge(rel_ready, s - (UNROLL - 1))
                            else:
                                sp.wait_ge(v_in[u], count(s, u, 16 * PER, -UNROLL))
                            sp.sem_inc(passed, 1)
                        sp.dma_start(dst_j[:, u, :], dst[bass.ds(e0, GE)].rearrange("(p j) -> p j", p=P)
                                     ).then_inc(dst_in[u], 16)
                        if window:
                            if at_least(s, UNROLL):
                                sp.wait_ge(v_made, s * 2 - (2 * UNROLL - 2))
                            sp.sem_inc(passed, 1)
                            row = sp.value_load(base_i[0:1, bass.ds(s, 1)], min_val=0, max_val=N - P)
                            sp.dma_start(v_win[:, u, :], v_tab[bass.ds(row, P), :]).then_inc(v_in[u], 16)

                    branches(sp, lambda: run_steps(sp, 0, UNROLL, UNROLL * (LAST // UNROLL) - 1, LAST, lambda s, u: load(s, u, True)),
                             lambda: run_steps(sp, 0, UNROLL, UNROLL * (LAST // UNROLL) - 1, LAST, lambda s, u: load(s, u, False)))

                @block.gpsimd
                def _(pool):
                    def gather(s, u):
                        pool.wait_ge(dst_in[u], count(s, u, 16))
                        if at_least(s, UNROLL):
                            pool.wait_ge(x_made, s * 2 - (2 * UNROLL - 2))
                        pool.sem_inc(passed, 1)
                        for j in range(PER):
                            pool.indirect_dma_start(v_rows[:, u, j, :], None, v_tab,
                                                    bass.IndirectOffsetOnAxis(dst_j[:, u, j:j + 1], 0)
                                                    ).then_inc(v_in[u], 16)

                    def scatter(s, u):
                        pool.wait_ge(row_chain, s * 4 + 4)
                        for j in range(PER):
                            if j % HALF == 0:
                                pool.wait_ge(x_copied, s * 2 + (j // HALF + 1))
                            r, k = j % COPIES, j // COPIES
                            if at_least(s, 1) or k:
                                pool.wait_ge(added[r], s * (16 * AC) + 16 * k)
                            pool.sem_inc(passed, 1)
                            pool.indirect_dma_start(acc[r], bass.IndirectOffsetOnAxis(row_i[:, u, j:j + 1], 0),
                                                    summed[:, u, j, :], None, compute_op=ALU.add
                                                    ).then_inc(added[r], 16)

                    def step(s, u):
                        if in_group(s, 1):
                            gather(s + 1, (u + 1) % UNROLL)
                        if at_least(s, 1):
                            scatter(s - 1, (u - 1) % UNROLL)

                    def with_window():
                        run_steps(pool, 0, UNROLL, UNROLL * (LAST // UNROLL) - 1, LAST, scatter)

                    def with_gather():
                        gather(0, 0)
                        run_steps(pool, 0, J0, J1, JLAST, step)

                    branches(pool, with_window, with_gather)
                    for r in range(COPIES):
                        pool.wait_ge(added[r], 16 * AC * NG)

                @block.tensor
                def _(pe):
                    def spread(s, u, window):
                        pe.wait_ge(prep, s * 2 + 2)
                        if at_least(s, 1):
                            pe.wait_ge(row_chain, s * 4 - 3)
                        for j in range(PER):
                            last = pe.matmul(ps_src[:, j, :], src_f[:, u, j:j + 1].to_broadcast([P, P]), ident[:],
                                             start=True, stop=True)
                        last.then_inc(spread_done, 1)
                        if window:
                            pe.wait_ge(rel_ready, s + 1)
                            if at_least(s, 1):
                                pe.wait_ge(one_ready, s)
                            for j in range(PER):
                                last = pe.matmul(ps_r[:, j, :], rel_j[:, u % 2, j:j + 1].to_broadcast([P, P]), ident_b[:],
                                                 start=True, stop=True)
                            last.then_inc(rel_spread, 1)

                    def values(s, u):
                        pe.wait_ge(one_ready, s + 1)
                        pe.wait_ge(v_in[u], count(s, u, 16))
                        for b in range(2):
                            if at_least(s, 1):
                                pe.wait_ge(v_copied, s * 2 - (1 - b))
                            for j in range(HALF * b, HALF * (b + 1)):
                                last = pe.matmul(ps_v[:, j, :], one_j[:, u % 2, j, :], v_win[:, u, :], start=True, stop=True)
                            last.then_inc(v_made, 1)

                    def combine(s, u, window):
                        pe.wait_ge(same_ready, s + 1)
                        if not window:
                            pe.wait_ge(v_in[u], count(s, u, 16 * PER))
                        for b in range(2):
                            if window:
                                pe.wait_ge(v_copied, s * 2 + (b + 1))
                            if at_least(s, 1):
                                pe.wait_ge(x_copied, s * 2 - (1 - b))
                            for j in range(HALF * b, HALF * (b + 1)):
                                last = pe.matmul(ps_x[:, j, :], same_w[:, u % 2, j, :], v_rows[:, u, j, :], start=True,
                                                 stop=True)
                            last.then_inc(x_made, 1)

                    def step(s, u, window):
                        if in_group(s, 1):
                            spread(s + 1, (u + 1) % UNROLL, window)
                        if window and in_group(s, 0):
                            values(s, u)
                        if at_least(s, 1):
                            combine(s - 1, (u - 1) % UNROLL, window)

                    def path(window):
                        spread(0, 0, window)
                        run_steps(pe, 0, J0, J1, JLAST, lambda s, u: step(s, u, window))

                    branches(pe, lambda: path(True), lambda: path(False))

                @block.scalar
                def _(act):
                    def copy_values(s, u):
                        for b in range(2):
                            act.wait_ge(v_made, s * 2 + (b + 1))
                            if at_least(s, UNROLL):
                                act.wait_ge(x_made, s * 2 - (2 * UNROLL - 1 - b))
                            h0, h1 = HALF * b, HALF * (b + 1)
                            nc.scalar.activation(v_rows[:, u, h0:h1, :], ps_v[:, h0:h1, :], ACT.Copy).then_inc(v_copied, 1)

                    def copy_sums(s, u):
                        for b in range(2):
                            act.wait_ge(x_made, s * 2 + (b + 1))
                            if b == 0 and at_least(s, UNROLL):
                                for r in range(COPIES):
                                    act.wait_ge(added[r], s * (16 * AC) - 16 * AC * (UNROLL - 1))
                            h0, h1 = HALF * b, HALF * (b + 1)
                            nc.scalar.activation(summed[:, u, h0:h1, :], ps_x[:, h0:h1, :], ACT.Copy).then_inc(x_copied, 1)

                    def step(s, u, window):
                        if window and in_group(s, 0):
                            copy_values(s, u)
                        if at_least(s, 1):
                            copy_sums(s - 1, (u - 1) % UNROLL)

                    branches(act, lambda: run_steps(act, 0, UNROLL + 1, UNROLL + UNROLL * ((NG - 2 - UNROLL) // UNROLL), JLAST,
                                                    lambda s, u: step(s, u, True)),
                             lambda: run_steps(act, 0, UNROLL + 1, UNROLL + UNROLL * ((NG - 2 - UNROLL) // UNROLL), JLAST,
                                               lambda s, u: step(s, u, False)))

                @block.vector
                def _(dve):
                    def prepare(s, u, window):
                        dve.wait_ge(src_in[u], count(s, u, 16))
                        if at_least(s, UNROLL):
                            dve.wait_ge(spread_done, s - (UNROLL - 1))
                        nc.vector.tensor_copy(src_f[:, u, :], src_j[:, u, :]).then_inc(prep, 1)
                        nc.vector.tensor_copy(w_now[:, u, :], weight[:, bass.ds(s * PER, PER)]).then_inc(prep, 1)
                        if window:
                            dve.wait_ge(dst_in[u], count(s, u, 16))
                            if at_least(s, 2):
                                dve.wait_ge(rel_spread, s - 1)
                            nc.vector.tensor_tensor(rel_j[:, u % 2, :], dst_j[:, u, :],
                                                    base_f[:, bass.ds(s, 1)].to_broadcast([P, PER]),
                                                    ALU.subtract).then_inc(rel_ready, 1)

                    def one_hot(s, u):
                        dve.wait_ge(rel_spread, s + 1)
                        if at_least(s, 2):
                            dve.wait_ge(v_made, s * 2 - 2)
                        nc.vector.tensor_scalar(one_j[:, u % 2, :, :], ps_r[:], part[:, 0:1], None,
                                                ALU.is_equal).then_inc(one_ready, 1)

                    def same(s, u):
                        dve.wait_ge(spread_done, s + 1)
                        dve.wait_ge(prep, s * 2 + 2)
                        if at_least(s, 2):
                            dve.wait_ge(x_made, s * 2 - 2)
                        for j in range(PER):
                            op = nc.vector.tensor_scalar(same_w[:, u % 2, j, :], ps_src[:, j, :], src_f[:, u, j:j + 1],
                                                         w_now[:, u, j:j + 1], ALU.is_equal, ALU.mult)
                        op.then_inc(same_ready, 1)
                        if at_least(s, UNROLL):
                            for r in range(COPIES):
                                dve.wait_ge(added[r], s * (16 * AC) - 16 * AC * (UNROLL - 1))
                        for j in range(PER):
                            op = nc.vector.scalar_tensor_tensor(same_b[:, j, :], ps_src[:, j, :], src_f[:, u, j:j + 1],
                                                                earlier[:], ALU.is_equal, ALU.mult,
                                                                accum_out=before[:, u, j:j + 1])
                        op.then_inc(row_chain, 1)
                        dve.wait_ge(row_chain, s * 4 + 1)
                        nc.vector.tensor_scalar(dup[:, u, :], before[:, u, :], 1.0, None, ALU.min).then_inc(row_chain, 1)
                        dve.wait_ge(row_chain, s * 4 + 2)
                        nc.vector.scalar_tensor_tensor(move[:, u, :], src_f[:, u, :], part[:, 1:2], dup[:, u, :],
                                                       ALU.subtract, ALU.mult).then_inc(row_chain, 1)
                        dve.wait_ge(row_chain, s * 4 + 3)
                        nc.vector.tensor_tensor(row_i[:, u, :], src_f[:, u, :], move[:, u, :],
                                                ALU.subtract).then_inc(row_chain, 1)

                    def step(s, u, window):
                        if in_group(s, 2):
                            prepare(s + 2, (u + 2) % UNROLL, window)
                        if in_group(s, 1):
                            if window:
                                one_hot(s + 1, (u + 1) % UNROLL)
                            same(s + 1, (u + 1) % UNROLL)

                    def path(window):
                        prepare(0, 0, window)
                        prepare(1, 1, window)
                        if window:
                            one_hot(0, 0)
                        same(0, 0)
                        run_steps(dve, 0, J0, J1, LAST, lambda s, u: step(s, u, window))

                    branches(dve, lambda: path(True), lambda: path(False))

        with ExitStack() as st:
            def tmp(name, shape, dt=F32):
                return st.enter_context(nc.sbuf_tensor(name, shape, dt))

            def sem(name):
                return st.enter_context(nc.semaphore(name))

            sums_in = tmp("sums_in", [P, 2, COPIES, NB, D])
            y_stats = tmp("y_stats", [P, 2, NB, 6])
            y_mv = tmp("y_mv", [P, 2, NB, 2])
            y_std = tmp("y_std", [P, 2, NB])
            y_rstd = tmp("y_rstd", [P, 2, NB])
            y_g = tmp("y_g", [P, 2, NB, D])
            o_sb = tmp("o_sb", [P, 2, NB, D])
            ps_y = st.enter_context(nc.psum_tensor("ps_y", [P, 2, NB, D], F32))

            acc_in = [sem("acc_in0"), sem("acc_in1")]
            y_ready = sem("y_ready")
            y_chain = sem("y_chain")
            y_std_ready = sem("y_std_ready")
            y_rstd_ready = sem("y_rstd_ready")
            y_g_ready = sem("y_g_ready")
            x_beta = sem("x_beta")
            o_ready = sem("o_ready")
            o_out = [sem("o_out0"), sem("o_out1")]

            def n_tiles(s):
                return 2 if known(s) and s == NSTEP else NB

            def final_steps(eng, step):
                for s in range(2):
                    step(s, s % 2)
                with eng.Fori(1, NSTEP // 2 - 1) as i:
                    for u in range(2):
                        step(i * 2 + u, u)
                for s in range(NSTEP - 2, NSTEP + 2):
                    step(s, s % 2)

            def upto(s, n):
                return (not known(s)) or s <= n

            with nc.Block() as block:
                @block.sync
                def _(sp):
                    def load(s, u):
                        if at_least(s, 2):
                            sp.wait_ge(y_ready, s - 1)
                        for r in range(COPIES):
                            if known(s) and s == NSTEP:
                                sp.dma_start(sums_in[:, u, r, 0:1, :], nodes_of(acc[r], s * NB, 1)).then_inc(acc_in[u], 16)
                                sp.dma_start(sums_in[0:NREM, u, r, 1, :], nodes_of(acc[r], TR, 1)).then_inc(acc_in[u], 16)
                            else:
                                sp.dma_start(sums_in[:, u, r, :, :], nodes_of(acc[r], s * NB, NB)).then_inc(acc_in[u], 16)

                    final_steps(sp, lambda s, u: load(s, u) if upto(s, NSTEP) else None)

                @block.gpsimd
                def _(pool):
                    with pool.Fori(0, NT) as t:
                        xt = x_sb[:, bass.ds(t, 1), :].rearrange("p a k -> p (a k)")
                        nc.gpsimd.tensor_tensor(xt, xt, beta_b[:], ALU.add).then_inc(x_beta, 1)

                @block.tensor
                def _(pe):
                    def add_up(s, u):
                        pe.wait_ge(acc_in[u], s * (8 * COPIES) + (16 * COPIES - u * 8 * COPIES)
                                   if n_tiles(s) == NB else NSTEP * 8 * COPIES + 32 * COPIES)
                        if at_least(s, 2):
                            pe.wait_ge(y_g_ready, (s - 1) * NB)
                        n = n_tiles(s)
                        y = ps_y[:, u, 0:n, :]
                        pe.matmul(y, ident[:], h_sb[:, bass.ds(s * NB, n), :], start=True, stop=False)
                        for r in range(COPIES):
                            last = pe.matmul(y, ident[:], sums_in[:, u, r, 0:n, :], start=False, stop=(r == COPIES - 1))
                        last.then_inc(y_ready, 1)

                    final_steps(pe, lambda s, u: add_up(s, u) if upto(s, NSTEP) else None)

                @block.scalar
                def _(act):
                    def root(s, u):
                        act.wait_ge(y_chain, (s + 1) * 2)
                        if at_least(s, 2):
                            act.wait_ge(y_rstd_ready, s - 1)
                        nc.scalar.activation(y_std[:, u, :], y_mv[:, u, :, 1], ACT.Sqrt, bias=eps[:, 0:1]
                                             ).then_inc(y_std_ready, 1)

                    def store(s, u):
                        act.wait_ge(o_ready, (s + 1) * NB if n_tiles(s) == NB else NSTEP * NB + 2)
                        if known(s) and s == NSTEP:
                            act.dma_start(nodes_of(out, s * NB, 1), o_sb[:, u, 0:1, :]).then_inc(o_out[u], 16)
                            act.dma_start(nodes_of(out, TR, 1), o_sb[0:NREM, u, 1, :]).then_inc(o_out[u], 16)
                        else:
                            act.dma_start(nodes_of(out, s * NB, NB), o_sb[:, u, :, :]).then_inc(o_out[u], 16)

                    def step(s, u):
                        if upto(s, NSTEP):
                            root(s, u)
                        if at_least(s, 1):
                            store(s - 1, 1 - u)

                    final_steps(act, step)
                    act.wait_ge(o_out[0], 16 * (NSTEP // 2) + 32)
                    act.wait_ge(o_out[1], 16 * (NSTEP // 2))

                @block.vector
                def _(dve):
                    def measure(s, u):
                        dve.wait_ge(y_ready, s + 1)
                        n = n_tiles(s)
                        for k in range(n):
                            op = nc.vector.bn_stats(y_stats[:, u, k, :], ps_y[:, u, k, :])
                        op.then_inc(y_chain, 1)
                        dve.wait_ge(y_chain, s * 2 + 1)
                        if at_least(s, 2):
                            dve.wait_ge(y_std_ready, s - 1)
                        dve.sem_inc(passed, 1)
                        for k in range(NB):
                            op = nc.vector.bn_aggr(y_mv[:, u, k, :], y_stats[:, u, k, :])
                        op.then_inc(y_chain, 1)

                    def finish(s, u):
                        dve.wait_ge(y_std_ready, s + 1)
                        nc.vector.reciprocal(y_rstd[:, u, :], y_std[:, u, :]).then_inc(y_rstd_ready, 1)
                        n = n_tiles(s)
                        for k in range(n):
                            nc.vector.scalar_tensor_tensor(y_g[:, u, k, :], ps_y[:, u, k, :], y_mv[:, u, k, 0:1], gamma_b[:],
                                                           ALU.subtract, ALU.mult).then_inc(y_g_ready, 1)
                        dve.wait_ge(y_rstd_ready, s + 1)
                        dve.wait_ge(x_beta, s * NB + n)
                        if at_least(s, 2):
                            dve.wait_ge(o_out[u], s * 8 - u * 8)
                        for k in range(n):
                            dve.wait_ge(y_g_ready, s * NB + (k + 1))
                            nc.vector.scalar_tensor_tensor(o_sb[:, u, k, :], y_g[:, u, k, :], y_rstd[:, u, k:k + 1],
                                                           x_sb[:, bass.ds(s * NB + k, 1), :].rearrange("p a k -> p (a k)"),
                                                           ALU.mult, ALU.add).then_inc(o_ready, 1)

                    def step(s, u):
                        if upto(s, NSTEP):
                            measure(s, u)
                        if at_least(s, 1):
                            finish(s - 1, 1 - u)

                    final_steps(dve, step)


NAMES = ["x", "src", "dst", "edge_attr_64"] + ["L0_gnn_" + n for n in (
    "Wn", "bn", "Wq", "bq", "Wk", "bk", "Wv", "bv", "We", "be", "A1", "b1", "A2", "b2", "gamma", "beta")]


def kernel(**inputs):
    import numpy as np
    import concourse.bacc as bacc
    from concourse.bass_utils import run_bass_kernel_spmd

    nc = bacc.Bacc("TRN2", target_bir_lowering=False, num_devices=1)
    arrays, args = {}, []
    for name in NAMES:
        a = np.ascontiguousarray(inputs[name])
        arrays[name + "_dram"] = a
        args.append(nc.dram_tensor(name + "_dram", a.shape, mybir.dt.from_np(a.dtype), kind="ExternalInput").ap())
    shape = arrays["x_dram"].shape
    args.append(nc.dram_tensor("out_dram", shape, F32, kind="ExternalOutput").ap())
    gnn_layer(nc, *args)
    r = run_bass_kernel_spmd(nc, [arrays], core_ids=[0])
    return r.results[0]["out_dram"]
```

```python
from contextlib import ExitStack

import concourse.bass as bass
from concourse import mybir

P = 128
PER = 8
GE = P * PER
UNROLL = 4
COPIES = 4
HALF = PER // 2
EPS = 1e-5
SLOPE = 0.2

ALU = mybir.AluOpType
ACT = mybir.ActivationFunctionType
F32 = mybir.dt.float32
BF16 = mybir.dt.bfloat16
I32 = mybir.dt.int32
AX_X = mybir.AxisListType.X
RMAX = bass.bass_isa.ReduceOp.max
RADD = bass.bass_isa.ReduceOp.add


def run_steps(eng, first, loop_from, loop_to, last, step):
    assert (loop_to + 1 - loop_from) % UNROLL == 0
    for s in range(first, loop_from):
        step(s, s % UNROLL)
    with eng.Fori(0, (loop_to + 1 - loop_from) // UNROLL) as i:
        for k in range(UNROLL):
            step(i * UNROLL + (loop_from + k), (loop_from + k) % UNROLL)
    for s in range(loop_to + 1, last + 1):
        step(s, s % UNROLL)


def known(s):
    return isinstance(s, int)


def at_least(s, n):
    return (not known(s)) or s >= n


def count(s, u, unit, ahead=0):
    g, v = s + ahead, (u + ahead) % UNROLL
    if known(s):
        return unit * (g // UNROLL + 1)
    return (g - v) * (unit // UNROLL) + unit


def gnn_layer(nc, x, src, dst, edge, Wn, bn, Wq, bq, Wk, bk, Wv, bv, We, be, A1, b1, A2, b2,
              gamma, beta, out):
    N, D = x.shape
    E, DE = edge.shape
    H = A2.shape[1]
    assert D == P and DE == P // 2
    FULL = E // GE
    LAST = FULL
    NG = FULL + 1
    TAIL0 = E - GE
    AGAIN = FULL * GE - TAIL0
    TR = N // P
    NREM = N - TR * P
    NT = TR + 1
    ROWS = -(-(N + P) // P) * P
    CH = -(-NG // P)
    assert E % GE and N % P

    q_tab = nc.dram_tensor("q_tab", [N, D], F32).ap()
    k_tab = nc.dram_tensor("k_tab", [N, D], F32).ap()
    v_tab = nc.dram_tensor("v_tab", [N, D], F32).ap()
    acc = [nc.dram_tensor(f"acc{r}", [ROWS, D], F32).ap() for r in range(COPIES)]

    def nodes_of(table, t, n, w=D):
        if known(t) and t == TR:
            return table[TR * P:N, :]
        return table[0:TR * P, :].rearrange("(p t) f -> p t f", t=TR)[:, bass.ds(t, n), :]

    with ExitStack() as ctx:
        def sb(name, shape, dt=F32):
            return ctx.enter_context(nc.sbuf_tensor(name, shape, dt))

        def sems(*names):
            return [ctx.enter_context(nc.semaphore(n)) for n in names]

        passed, = sems("passed")

        zeros = sb("zeros", [P, D])
        eps = sb("eps", [P, 1])
        ident = sb("ident", [P, P])
        ident_b = sb("ident_b", [P, P], BF16)
        earlier = sb("earlier", [P, P])
        part_i = sb("part_i", [P, 2], I32)
        part = sb("part", [P, 2])
        tail_mask = sb("tail_mask", [P, PER])
        x_sb = sb("x_sb", [P, NT, D])
        h_sb = sb("h_sb", [P, NT, D])
        w2 = sb("w2", [P, D])
        a2 = sb("a2", [P, H])
        b2_rep = sb("b2_rep", [P, PER, H])
        gamma_b = sb("gamma_b", [P, D])
        beta_b = sb("beta_b", [P, D])
        base_neg = sb("base_neg", [P, CH * P])
        base_i = sb("base_i", [P, CH * P], I32)
        local_i = sb("local_i", [P, 1], I32)
        score = sb("score", [P, NG * PER])
        weight = sb("weight", [P, NG * PER])

        NB = 4
        NSTEP = TR // NB
        assert TR % NB == 1
        with ExitStack() as st:
            def tmp(name, shape, dt=F32):
                return st.enter_context(nc.sbuf_tensor(name, shape, dt))

            def psum(name, shape):
                return st.enter_context(nc.psum_tensor(name, shape, F32))

            def sem(name):
                return st.enter_context(nc.semaphore(name))

            wm = tmp("wm", [P, 4 * D])
            bias = tmp("bias", [P, 4 * D])
            wq = tmp("wq", [P, D])
            wk = tmp("wk", [P, D])
            we = tmp("we", [DE, D])
            a1 = tmp("a1", [P, 3, D])
            bcol = tmp("bcol", [P, 3])
            b2_b = tmp("b2_b", [P, H])
            wqT = tmp("wqT", [P, D])
            wkT = tmp("wkT", [P, D])
            weT = tmp("weT", [P, 2, DE])
            stats = tmp("stats", [P, UNROLL, NB, 6])
            mv = tmp("mv", [P, UNROLL, NB, 2])
            std = tmp("std", [P, NT])
            rstd = tmp("rstd", [P, NT])
            shift_x = tmp("shift_x", [P, NT])
            xn = tmp("xn", [P, 2, NB, D])
            hT = tmp("hT", [P, 2, NB * P])
            tabs = tmp("tabs", [P, 2, 3, NB, D])
            dgroup = tmp("dgroup", [P, CH, GE], I32)
            dmin = tmp("dmin", [P, CH])
            dmax = tmp("dmax", [P, CH])
            dspan = tmp("dspan", [P, CH])
            span_row = tmp("span_row", [P, CH * P])
            span = tmp("span", [P, 1])
            ps_t = psum("ps_t", [P, 2, 512])
            ps_m = psum("ps_m", [P, NB, 512])
            ps_w = psum("ps_w", [P, 2, 512])

            made = sem("made")
            w_in = sem("w_in")
            x_in = [sem(f"x_in{u}") for u in range(UNROLL)]
            d_in = sem("d_in")
            w_turned = sem("w_turned")
            w_copied = sem("w_copied")
            w_made = sem("w_made")
            ready = sem("ready")
            stat_chain = sem("stat_chain")
            std_ready = sem("std_ready")
            scale_chain = sem("scale_chain")
            xn_ready = sem("xn_ready")
            turned = sem("turned")
            hT_ready = sem("hT_ready")
            m_ready = sem("m_ready")
            tab_ready = sem("tab_ready")
            stored = [sem("stored0"), sem("stored1")]
            span_chain = sem("span_chain")
            span_turned = sem("span_turned")

            N_MADE = 12
            LOADS = 16

            def tiles(s):
                return 2 if known(s) and s == NSTEP else NB

            def upto_last(s):
                return (not known(s)) or 0 <= s <= NSTEP

            def node_steps(eng, step):
                run_steps(eng, -3, 1, 16, NSTEP, step)

            with nc.Block() as block:
                @block.gpsimd
                def _(pool):
                    nc.gpsimd.memset(x_sb[:, TR, :], 0.0).then_inc(made, 1)
                    nc.gpsimd.memset(dgroup[:, CH - 1, :], 0).then_inc(made, 1)
                    nc.gpsimd.memset(eps[:], EPS).then_inc(made, 1)
                    nc.gpsimd.memset(ident[:], 0.0).then_inc(made, 1)
                    nc.gpsimd.memset(earlier[:], 1.0).then_inc(made, 1)
                    nc.gpsimd.memset(tail_mask[:], 1.0).then_inc(made, 1)
                    nc.gpsimd.memset(zeros[:], 0.0).then_inc(made, 1)
                    pool.wait_ge(made, 7)
                    nc.gpsimd.affine_select(out=ident[:], in_=ident[:], compare_op=ALU.not_equal, fill=1.0,
                                            base=0, pattern=[[-1, P]], channel_multiplier=1).then_inc(made, 1)
                    nc.gpsimd.affine_select(out=earlier[:], in_=earlier[:], compare_op=ALU.is_gt, fill=0.0,
                                            base=0, pattern=[[-1, P]], channel_multiplier=1).then_inc(made, 1)
                    nc.gpsimd.affine_select(out=tail_mask[:], in_=tail_mask[:], compare_op=ALU.is_ge, fill=0.0,
                                            base=-AGAIN, pattern=[[1, PER]], channel_multiplier=PER).then_inc(made, 1)
                    nc.gpsimd.iota(part_i[:, 0:1], [[0, 1]], base=0, channel_multiplier=1).then_inc(made, 1)
                    nc.gpsimd.iota(part_i[:, 1:2], [[0, 1]], base=N, channel_multiplier=1).then_inc(made, 1)

                @block.sync
                def _(sp):
                    row = lambda v: v.rearrange("(a d) -> a d", a=1).to_broadcast([P, v.shape[0]])
                    col = lambda v: v.rearrange("(d a) -> d a", a=1)

                    def load_x(s, u):
                        if known(s) and s == NSTEP:
                            sp.wait_ge(made, 7)
                            sp.dma_start(x_sb[:, s * NB:s * NB + 1, :], nodes_of(x, s * NB, 1)).then_inc(x_in[u], 16)
                            sp.dma_start(x_sb[0:NREM, TR, :], nodes_of(x, TR, 1)).then_inc(x_in[u], 16)
                        else:
                            sp.dma_start(x_sb[:, bass.ds(s * NB, NB), :], nodes_of(x, s * NB, NB)).then_inc(x_in[u], 16)

                    loads = [
                        (wq[:], Wq), (wk[:], Wk), (we[:], We),
                        (a1[:], A1.rearrange("(c p) f -> p c f", p=P)),
                        (bcol[:, 0:1], col(bq)), (bcol[:, 1:2], col(bk)), (bcol[:, 2:3], col(be)),
                        (wm[:, 0:D], Wn), (wm[:, 3 * D:4 * D], Wv), (a2[:], A2),
                        (bias[:, 0:D], row(bn)), (bias[:, 2 * D:3 * D], row(b1)), (bias[:, 3 * D:4 * D], row(bv)),
                        (b2_b[:], row(b2)), (gamma_b[:], row(gamma)), (beta_b[:], row(beta)),
                    ]
                    assert len(loads) == LOADS
                    load_x(0, 0)
                    for d, s in loads[:7]:
                        sp.dma_start(d, s).then_inc(w_in, 16)
                    load_x(1, 1)
                    for d, s in loads[7:]:
                        sp.dma_start(d, s).then_inc(w_in, 16)
                    load_x(2, 2)
                    load_x(3, 3)
                    for c in range(CH - 1):
                        sp.dma_start(dgroup[:, c, :], dst[c * P * GE:(c + 1) * P * GE].rearrange("(g e) -> g e", g=P)
                                     ).then_inc(d_in, 16)
                    sp.wait_ge(made, 7)
                    rest = FULL - (CH - 1) * P
                    sp.dma_start(dgroup[0:rest, CH - 1, :],
                                 dst[(CH - 1) * P * GE:FULL * GE].rearrange("(g e) -> g e", g=rest)).then_inc(d_in, 16)
                    sp.dma_start(dgroup[rest:rest + 1, CH - 1, :],
                                 dst[TAIL0:E].rearrange("(g e) -> g e", g=1)).then_inc(d_in, 16)

                    def step(s, u):
                        if upto_last(s + 3 + UNROLL):
                            sp.wait_ge(stat_chain, s * 2 + 7)
                            load_x(s + 3 + UNROLL, (u + 3) % UNROLL)
                        if known(s) and s < 0:
                            return
                        sp.wait_ge(tab_ready, s * (2 * NB) + 2 * tiles(s))
                        for i, table in enumerate((q_tab, k_tab, v_tab)):
                            if tiles(s) == NB:
                                sp.dma_start(nodes_of(table, s * NB, NB), tabs[:, u % 2, i, :, :]).then_inc(stored[u % 2], 16)
                            else:
                                sp.dma_start(nodes_of(table, s * NB, 1), tabs[:, u % 2, i, 0:1, :]).then_inc(stored[u % 2], 16)
                                sp.dma_start(nodes_of(table, TR, 1), tabs[0:NREM, u % 2, i, 1, :]).then_inc(stored[u % 2], 16)

                    node_steps(sp, step)
                    sp.wait_ge(stored[0], 48 * (NSTEP // 2) + 96)
                    sp.wait_ge(stored[1], 48 * (NSTEP // 2))

                @block.tensor
                def _(pe):
                    pe.wait_ge(made, N_MADE)
                    pe.wait_ge(w_in, 16 * LOADS)
                    pe.transpose(ps_w[:, 0, 0:P], wq[:], ident[:])
                    pe.transpose(ps_w[:, 0, P:2 * P], wk[:], ident[:])
                    pe.transpose(ps_w[:, 0, 2 * P:2 * P + DE], we[:], ident[0:DE, 0:DE]).then_inc(w_turned, 1)
                    pe.wait_ge(w_copied, 4)
                    pe.matmul(ps_w[:, 1, 0:P], wqT[:], a1[:, 0, :], start=True, stop=True)
                    pe.matmul(ps_w[:, 1, P:2 * P], wkT[:], a1[:, 1, :], start=True, stop=True)
                    pe.matmul(ps_w[:, 1, 2 * P:3 * P], weT[:].rearrange("p a k -> p (a k)"), a1[:, 2, :],
                              start=True, stop=True)
                    pe.matmul(ps_w[:, 0, 0:P], bcol[:, 0:1].to_broadcast([P, P]), a1[:, 0, :], start=True, stop=True)
                    pe.matmul(ps_w[:, 0, P:2 * P], bcol[:, 1:2].to_broadcast([P, P]), a1[:, 1, :], start=True, stop=False)
                    pe.matmul(ps_w[:, 0, P:2 * P], bcol[:, 2:3].to_broadcast([P, P]), a1[:, 2, :], start=False,
                              stop=True).then_inc(w_made, 1)
                    pe.wait_ge(ready, 6 + PER)

                    def turn(s, u):
                        pe.wait_ge(xn_ready, s + 1)
                        if at_least(s, 2):
                            pe.wait_ge(hT_ready, s - 1)
                        for k in range(tiles(s)):
                            last = pe.transpose(ps_t[:, u % 2, k * P:(k + 1) * P], xn[:, u % 2, k, :], ident[:])
                        last.then_inc(turned, 1)

                    def project(s, u):
                        pe.wait_ge(hT_ready, s + 1)
                        for k in range(tiles(s)):
                            if at_least(s, 1):
                                pe.wait_ge(tab_ready, s * (2 * NB) - 2 * (NB - 1 - k))
                            pe.matmul(ps_m[:, k, :], hT[:, u % 2, k * P:(k + 1) * P], wm[:], start=True,
                                      stop=True).then_inc(m_ready, 1)

                    def step(s, u):
                        if upto_last(s + 1):
                            turn(s + 1, u + 1)
                        if upto_last(s):
                            project(s, u)

                    node_steps(pe, step)
                    pe.wait_ge(span_chain, 4)
                    for c in range(CH):
                        pe.matmul(ps_w[:, 0, c * P:(c + 1) * P], dmin[:, c:c + 1].to_broadcast([P, P]), ident[:],
                                  start=True, stop=True)
                        last = pe.matmul(ps_w[:, 1, c * P:(c + 1) * P], dspan[:, c:c + 1].to_broadcast([P, P]), ident[:],
                                         start=True, stop=True)
                    last.then_inc(span_turned, 1)

                @block.scalar
                def _(act):
                    act.wait_ge(made, 3)

                    def root(s, u):
                        act.wait_ge(stat_chain, s * 2 + 2)
                        t, n = s * NB, tiles(s)
                        nc.scalar.activation(std[:, bass.ds(t, n)], mv[:, u, 0:n, 1], ACT.Sqrt,
                                             bias=eps[:, 0:1]).then_inc(std_ready, 1)

                    def normal(s, u):
                        act.wait_ge(scale_chain, s * 2 + 2)
                        if at_least(s, 2):
                            act.wait_ge(turned, s - 1)
                        for k in range(tiles(s)):
                            t = s * NB + k
                            op = nc.scalar.activation(xn[:, u % 2, k, :], x_sb[:, bass.ds(t, 1), :].rearrange("p a k -> p (a k)"),
                                                      ACT.Identity, scale=rstd[:, bass.ds(t, 1)], bias=shift_x[:, bass.ds(t, 1)])
                        op.then_inc(xn_ready, 1)

                    def relu(s, u):
                        act.wait_ge(turned, s + 1)
                        if at_least(s, 2):
                            act.wait_ge(m_ready, (s - 1) * NB)
                        w = tiles(s) * P
                        nc.scalar.activation(hT[:, u % 2, 0:w], ps_t[:, u % 2, 0:w], ACT.Relu).then_inc(hT_ready, 1)

                    def step(s, u):
                        if upto_last(s + 1):
                            relu(s + 1, u + 1)
                        if upto_last(s + 2):
                            normal(s + 2, u)
                        if upto_last(s + 3):
                            root(s + 3, (u + 3) % UNROLL)

                    node_steps(act, step)

                @block.vector
                def _(dve):
                    def stats_of(s, u):
                        dve.wait_ge(x_in[u], count(s, u, 16) if tiles(s) == NB else count(s, u, 16) + 16)
                        for k in range(tiles(s)):
                            t = s * NB + k
                            op = nc.vector.bn_stats(stats[:, u, k, :], x_sb[:, bass.ds(t, 1), :].rearrange("p a k -> p (a k)"))
                        op.then_inc(stat_chain, 1)
                        dve.wait_ge(stat_chain, s * 2 + 1)
                        dve.sem_inc(passed, 1)
                        for k in range(tiles(s)):
                            t = s * NB + k
                            op = nc.vector.bn_aggr(mv[:, u, k, :], stats[:, u, k, :])
                        op.then_inc(stat_chain, 1)

                    def scale_of(s, u):
                        dve.wait_ge(std_ready, s + 1)
                        t, n = s * NB, tiles(s)
                        nc.vector.reciprocal(rstd[:, bass.ds(t, n)], std[:, bass.ds(t, n)]).then_inc(scale_chain, 1)
                        dve.wait_ge(scale_chain, s * 2 + 1)
                        nc.vector.scalar_tensor_tensor(shift_x[:, bass.ds(t, n)], mv[:, u, 0:n, 0], -1.0,
                                                       rstd[:, bass.ds(t, n)], ALU.mult, ALU.mult).then_inc(scale_chain, 1)

                    def add_bias(s, u):
                        if at_least(s, 2):
                            dve.wait_ge(stored[u % 2], (s - u % 2) * 24)
                        for k in range(tiles(s)):
                            dve.wait_ge(m_ready, s * NB + (k + 1))
                            nc.vector.tensor_tensor(h_sb[:, bass.ds(s * NB + k, 1), :].rearrange("p a k -> p (a k)"),
                                                    ps_m[:, k, 0:D], bias[:, 0:D], ALU.add).then_inc(tab_ready, 1)
                            nc.vector.tensor_tensor(tabs[:, u % 2, :, k, :], ps_m[:, k, D:4 * D].rearrange("p (a f) -> p a f", a=3),
                                                    bias[:, D:4 * D].rearrange("p (a f) -> p a f", a=3),
                                                    ALU.add).then_inc(tab_ready, 1)

                    def weights_of():
                        dve.wait_ge(w_turned, 1)
                        nc.vector.tensor_copy(wqT[:], ps_w[:, 0, 0:P]).then_inc(w_copied, 1)
                        nc.vector.tensor_copy(wkT[:], ps_w[:, 0, P:2 * P]).then_inc(w_copied, 1)
                        nc.vector.tensor_copy(weT[:, 0, :], ps_w[:, 0, 2 * P:2 * P + DE]).then_inc(w_copied, 1)
                        nc.vector.tensor_copy(weT[:, 1, :], ps_w[:, 0, 2 * P:2 * P + DE]).then_inc(w_copied, 1)
                        dve.wait_ge(w_made, 1)
                        nc.vector.tensor_copy(wm[:, D:3 * D], ps_w[:, 1, 0:2 * D]).then_inc(ready, 1)
                        nc.vector.tensor_copy(w2[:], ps_w[:, 1, 2 * D:3 * D]).then_inc(ready, 1)
                        nc.vector.tensor_copy(bias[:, D:2 * D], ps_w[:, 0, 0:D]).then_inc(ready, 1)
                        nc.vector.tensor_tensor(bias[:, 2 * D:3 * D], bias[:, 2 * D:3 * D], ps_w[:, 0, D:2 * D],
                                                ALU.add).then_inc(ready, 1)
                        for j in range(PER):
                            nc.vector.tensor_copy(b2_rep[:, j, :], b2_b[:]).then_inc(ready, 1)
                        nc.vector.tensor_copy(part[:], part_i[:]).then_inc(ready, 1)
                        nc.vector.tensor_copy(ident_b[:], ident[:]).then_inc(ready, 1)
                        dve.wait_ge(ready, 6 + PER)

                    def step(s, u):
                        if upto_last(s + 2):
                            scale_of(s + 2, (u + 2) % UNROLL)
                        if upto_last(s + 3):
                            stats_of(s + 3, (u + 3) % UNROLL)
                        if known(s) and s == -1:
                            weights_of()
                        if upto_last(s):
                            add_bias(s, u)

                    node_steps(dve, step)
                    dve.wait_ge(d_in, 16 * (CH + 1))
                    nc.vector.tensor_reduce(dmin[:], dgroup[:], AX_X, ALU.min).then_inc(span_chain, 1)
                    nc.vector.tensor_reduce(dmax[:], dgroup[:], AX_X, ALU.max).then_inc(span_chain, 1)
                    dve.wait_ge(span_chain, 2)
                    nc.vector.tensor_scalar(dmin[:], dmin[:], float(N - P), None, ALU.min).then_inc(span_chain, 1)
                    dve.wait_ge(span_chain, 3)
                    nc.vector.tensor_tensor(dspan[:], dmax[:], dmin[:], ALU.subtract).then_inc(span_chain, 1)
                    dve.wait_ge(span_turned, 1)
                    nc.vector.tensor_scalar(base_neg[:], ps_w[:, 0, 0:CH * P], -1.0, None, ALU.mult).then_inc(span_chain, 1)
                    nc.vector.tensor_copy(base_i[:], ps_w[:, 0, 0:CH * P]).then_inc(span_chain, 1)
                    nc.vector.tensor_reduce(span[:], ps_w[:, 1, 0:CH * P], AX_X, ALU.max).then_inc(span_chain, 1)
                    dve.wait_ge(span_chain, 7)
                    nc.vector.tensor_scalar(local_i[:], span[:], float(P - 1), None, ALU.is_le).then_inc(span_chain, 1)

        def group_edges(s):
            return TAIL0 if known(s) and s == LAST else s * GE

        L0, L1 = 3, 3 + UNROLL * ((NG - 1 - 3 - 1) // UNROLL) - 1
        LASTSTEP = NG

        def branches(eng, with_window, with_gather):
            flag = eng.value_load(local_i[0:1, 0:1], min_val=0, max_val=1)
            with eng.If(flag):
                with_window()
            with eng.Else():
                with_gather()

        def in_group(s, n):
            return (not known(s)) or 0 <= s + n < NG

        with ExitStack() as st:
            def tmp(name, shape, dt=F32):
                return st.enter_context(nc.sbuf_tensor(name, shape, dt))

            def psum(name, shape):
                return st.enter_context(nc.psum_tensor(name, shape, F32))

            def sem(name):
                return st.enter_context(nc.semaphore(name))

            edges = tmp("edges", [P, UNROLL, PER, DE])
            src_i = tmp("src_i", [P, UNROLL, PER], I32)
            dst_i = tmp("dst_i", [P, UNROLL, PER], I32)
            q_rows = tmp("q_rows", [P, UNROLL, PER, D])
            k_rows = tmp("k_rows", [P, UNROLL, PER, D])
            k_win = k_rows
            rel = tmp("rel", [P, 2, PER], BF16)
            onehot = tmp("onehot", [P, 2, PER, P])
            edgeT = tmp("edgeT", [P, 2, HALF, P])
            low = tmp("low", [P, 2, PER, P])
            mid = tmp("mid", [P, 2, PER, P])
            head = tmp("head", [P, 2, PER, H])
            head2 = tmp("head2", [P, 2, PER, H])
            ps_rel = psum("ps_rel", [P, PER, P])
            ps_z = psum("ps_z", [P, 2, PER, P])
            ps_e = psum("ps_e", [P, HALF, P])
            ps_s = psum("ps_s", [P, 2, PER, H])

            zeroed = sem("zeroed")
            edges_in = [sem(f"edges_in{u}") for u in range(UNROLL)]
            src_in = [sem(f"src_in{u}") for u in range(UNROLL)]
            dst_in = [sem(f"dst_in{u}") for u in range(UNROLL)]
            q_in = [sem(f"q_in{u}") for u in range(UNROLL)]
            k_in = [sem(f"k_in{u}") for u in range(UNROLL)]
            edge_turned = sem("edge_turned")
            edgeT_ready = sem("edgeT_ready")
            rel_ready = sem("rel_ready")
            rel_spread = sem("rel_spread")
            onehot_ready = sem("onehot_ready")
            z_ready = sem("z_ready")
            low_ready = sem("low_ready")
            mid_ready = sem("mid_ready")
            s_ready = sem("s_ready")
            score_chain = sem("score_chain")

            def tile_at(b, k):
                return 2 * k + b

            with nc.Block() as block:
                @block.sync
                def _(sp):
                    LOOPS = LAST // UNROLL - 1

                    def zero(block_of_rows):
                        for r in range(COPIES):
                            sp.dma_start(acc[r][bass.ds(block_of_rows * P, P), :], zeros[:]).then_inc(zeroed, 16)

                    def load(s, u, window):
                        if not known(s) and u == 0:
                            zero((s - UNROLL) // UNROLL)
                        e0 = group_edges(s)
                        if at_least(s, UNROLL):
                            sp.wait_ge(edge_turned, s - (UNROLL - 1))
                            sp.sem_inc(passed, 1)
                        sp.dma_start(edges[:, u, :, :], edge[bass.ds(e0, GE), :].rearrange("(p j) f -> p j f", p=P)
                                     ).then_inc(edges_in[u], 16)
                        if at_least(s, UNROLL):
                            sp.wait_ge(q_in[u], count(s, u, 16 * PER, -UNROLL))
                            sp.sem_inc(passed, 1)
                        sp.dma_start(src_i[:, u, :], src[bass.ds(e0, GE)].rearrange("(p j) -> p j", p=P)
                                     ).then_inc(src_in[u], 16)
                        if at_least(s, UNROLL):
                            if window:
                                sp.wait_ge(rel_ready, s - (UNROLL - 1))
                            else:
                                sp.wait_ge(k_in[u], count(s, u, 16 * PER, -UNROLL))
                            sp.sem_inc(passed, 1)
                        sp.dma_start(dst_i[:, u, :], dst[bass.ds(e0, GE)].rearrange("(p j) -> p j", p=P)
                                     ).then_inc(dst_in[u], 16)
                        if window:
                            if at_least(s, UNROLL):
                                sp.wait_ge(z_ready, s * 2 - (2 * UNROLL - 2))
                            sp.sem_inc(passed, 1)
                            row = sp.value_load(base_i[0:1, bass.ds(s, 1)], min_val=0, max_val=N - P)
                            sp.dma_start(k_win[:, u, 0, :], k_tab[bass.ds(row, P), :]).then_inc(k_in[u], 16)

                    branches(sp, lambda: run_steps(sp, 0, UNROLL, UNROLL * (LAST // UNROLL) - 1, LAST, lambda s, u: load(s, u, True)),
                             lambda: run_steps(sp, 0, UNROLL, UNROLL * (LAST // UNROLL) - 1, LAST, lambda s, u: load(s, u, False)))
                    for rows in range(LOOPS, ROWS // P):
                        zero(rows)
                    sp.wait_ge(zeroed, 16 * COPIES * (ROWS // P))

                @block.gpsimd
                def _(pool):
                    def gather(s, u, window):
                        pool.wait_ge(src_in[u], count(s, u, 16))
                        if at_least(s, UNROLL):
                            pool.wait_ge(z_ready, s * 2 - (2 * UNROLL - 2))
                        pool.sem_inc(passed, 1)
                        for j in range(PER):
                            pool.indirect_dma_start(q_rows[:, u, j, :], None, q_tab,
                                                    bass.IndirectOffsetOnAxis(src_i[:, u, j:j + 1], 0)
                                                    ).then_inc(q_in[u], 16)
                        if not window:
                            pool.wait_ge(dst_in[u], count(s, u, 16))
                            pool.sem_inc(passed, 1)
                            for j in range(PER):
                                pool.indirect_dma_start(k_rows[:, u, j, :], None, k_tab,
                                                        bass.IndirectOffsetOnAxis(dst_i[:, u, j:j + 1], 0)
                                                        ).then_inc(k_in[u], 16)

                    branches(pool, lambda: run_steps(pool, 0, UNROLL, UNROLL * (LAST // UNROLL) - 1, LAST, lambda s, u: gather(s, u, True)),
                             lambda: run_steps(pool, 0, UNROLL, UNROLL * (LAST // UNROLL) - 1, LAST, lambda s, u: gather(s, u, False)))

                @block.tensor
                def _(pe):
                    def turn(s, u):
                        pe.wait_ge(edges_in[u], count(s, u, 16))
                        if at_least(s, 1):
                            pe.wait_ge(edgeT_ready, s)
                        for k in range(HALF):
                            last = pe.transpose(ps_e[:, k, :], edges[:, u, 2 * k:2 * k + 2, :].rearrange("p j f -> p (j f)"),
                                                ident[:])
                        last.then_inc(edge_turned, 1)

                    def spread(s, u):
                        pe.wait_ge(rel_ready, s + 1)
                        if at_least(s, 1):
                            pe.wait_ge(onehot_ready, s)
                        for b in range(2):
                            for k in range(HALF):
                                last = pe.matmul(ps_rel[:, HALF * b + k, :],
                                                 rel[:, u % 2, tile_at(b, k):tile_at(b, k) + 1].to_broadcast([P, P]),
                                                 ident_b[:], start=True, stop=True)
                        last.then_inc(rel_spread, 1)

                    def make_z(s, u, window):
                        pe.wait_ge(edgeT_ready, s + 1)
                        pe.wait_ge(k_in[u], count(s, u, 16 if window else 16 * PER))
                        if window:
                            pe.wait_ge(onehot_ready, s + 1)
                        if at_least(s, 2):
                            pe.wait_ge(mid_ready, s * 2 - 2)
                        for b in range(2):
                            bank = ps_z[:, u % 2, HALF * b:HALF * (b + 1), :]
                            lo = DE * b
                            pe.matmul(bank.rearrange("p k e -> p (k e)"), w2[lo:lo + DE, :],
                                      edgeT[lo:lo + DE, u % 2, :, :].rearrange("p k e -> p (k e)"),
                                      start=True, stop=False, skip_group_check=True)
                            if window:
                                pe.matmul(bank.rearrange("p k e -> p (k e)"), k_win[:, u, 0, :],
                                          onehot[:, u % 2, HALF * b:HALF * (b + 1), :].rearrange("p k e -> p (k e)"),
                                          start=False, stop=False, skip_group_check=True)
                            if b == 0:
                                pe.wait_ge(q_in[u], count(s, u, 16 * PER))
                            for k in range(HALF):
                                if not window:
                                    pe.matmul(ps_z[:, u % 2, HALF * b + k, :], k_rows[:, u, tile_at(b, k), :], ident[:],
                                              start=False, stop=False, skip_group_check=True)
                                last = pe.matmul(ps_z[:, u % 2, HALF * b + k, :], q_rows[:, u, tile_at(b, k), :], ident[:],
                                                 start=False, stop=(k == HALF - 1), skip_group_check=True)
                            last.then_inc(z_ready, 1)

                    def heads(s, u):
                        pe.wait_ge(mid_ready, s * 2 + 2)
                        if at_least(s, 1):
                            pe.wait_ge(score_chain, s * 3 - 2)
                        for b in range(2):
                            for k in range(HALF):
                                last = pe.matmul(ps_s[:, u % 2, tile_at(b, k), :], mid[:, u % 2, HALF * b + k, :], a2[:],
                                                 start=True, stop=True)
                        last.then_inc(s_ready, 1)

                    def step(s, u, window):
                        if in_group(s, 1):
                            turn(s + 1, (u + 1) % UNROLL)
                            if window:
                                spread(s + 1, (u + 1) % UNROLL)
                        if in_group(s, 0):
                            make_z(s, u, window)
                        if at_least(s, 1):
                            heads(s - 1, (u - 1) % UNROLL)

                    def path(window):
                        turn(0, 0)
                        if window:
                            spread(0, 0)
                        run_steps(pe, 0, L0, L1, LASTSTEP, lambda s, u: step(s, u, window))

                    branches(pe, lambda: path(True), lambda: path(False))

                @block.scalar
                def _(act):
                    def copy_edges(s, u):
                        act.wait_ge(edge_turned, s + 1)
                        if at_least(s, 2):
                            act.wait_ge(z_ready, s * 2 - 2)
                        nc.scalar.activation(edgeT[:, u % 2, :, :], ps_e[:], ACT.Copy).then_inc(edgeT_ready, 1)

                    def scale(s, u):
                        for b in range(2):
                            act.wait_ge(z_ready, s * 2 + (b + 1))
                            if at_least(s, 2):
                                act.wait_ge(mid_ready, s * 2 - (3 - b))
                            h0, h1 = HALF * b, HALF * (b + 1)
                            nc.scalar.activation(low[:, u % 2, h0:h1, :], ps_z[:, u % 2, h0:h1, :], ACT.Copy,
                                                 scale=SLOPE).then_inc(low_ready, 1)

                    def step(s, u):
                        if in_group(s, 1):
                            copy_edges(s + 1, (u + 1) % UNROLL)
                        if in_group(s, 0):
                            scale(s, u)

                    copy_edges(0, 0)
                    run_steps(act, 0, L0, L1, LAST, step)

                @block.vector
                def _(dve):
                    def relative(s, u):
                        dve.wait_ge(dst_in[u], count(s, u, 16))
                        if at_least(s, 2):
                            dve.wait_ge(rel_spread, s - 1)
                        nc.vector.tensor_tensor(rel[:, u % 2, :], dst_i[:, u, :], base_neg[:, bass.ds(s, 1)].to_broadcast([P, PER]),
                                                ALU.add).then_inc(rel_ready, 1)

                    def one_hot(s, u):
                        dve.wait_ge(rel_spread, s + 1)
                        if at_least(s, 2):
                            dve.wait_ge(z_ready, s * 2 - 2)
                        nc.vector.tensor_scalar(onehot[:, u % 2, :, :], ps_rel[:], part[:, 0:1], None,
                                                ALU.is_equal).then_inc(onehot_ready, 1)

                    def leaky(s, u):
                        if at_least(s, 2):
                            dve.wait_ge(s_ready, s - 1)
                        for b in range(2):
                            dve.wait_ge(low_ready, s * 2 + (b + 1))
                            h0, h1 = HALF * b, HALF * (b + 1)
                            nc.vector.tensor_tensor(mid[:, u % 2, h0:h1, :], low[:, u % 2, h0:h1, :],
                                                    ps_z[:, u % 2, h0:h1, :], ALU.max).then_inc(mid_ready, 1)

                    def head_sum(s, u):
                        dve.wait_ge(s_ready, s + 1)
                        nc.vector.tensor_tensor(head[:, u % 2, :, :], ps_s[:, u % 2, :, :], b2_rep[:],
                                                ALU.add).then_inc(score_chain, 1)
                        dve.wait_ge(score_chain, s * 3 + 1)
                        nc.vector.scalar_tensor_tensor(head2[:, u % 2, :, :], head[:, u % 2, :, :], SLOPE,
                                                       head[:, u % 2, :, :], ALU.mult, ALU.max).then_inc(score_chain, 1)
                        dve.wait_ge(score_chain, s * 3 + 2)
                        nc.vector.tensor_reduce(score[:, bass.ds(s * PER, PER)], head2[:, u % 2, :, :], AX_X,
                                                ALU.add).then_inc(score_chain, 1)

                    def step(s, u, window):
                        if window:
                            if in_group(s, 2):
                                relative(s + 2, (u + 2) % UNROLL)
                            if in_group(s, 1):
                                one_hot(s + 1, (u + 1) % UNROLL)
                        if in_group(s, 0):
                            leaky(s, u)
                        if at_least(s, 1):
                            head_sum(s - 1, (u - 1) % UNROLL)

                    def path(window):
                        if window:
                            relative(0, 0)
                            relative(1, 1)
                            one_hot(0, 0)
                        run_steps(dve, 0, L0, L1, LASTSTEP, lambda s, u: step(s, u, window))

                    branches(dve, lambda: path(True), lambda: path(False))

        with ExitStack() as st:
            def tmp(name, shape, dt=F32):
                return st.enter_context(nc.sbuf_tensor(name, shape, dt))

            def sem(name):
                return st.enter_context(nc.semaphore(name))

            top = tmp("top", [P, 1])
            top_all = tmp("top_all", [P, 1])
            shift = tmp("shift", [P, 1])
            sums = tmp("sums", [P, 2])
            total = tmp("total", [P, 1])
            total_all = tmp("total_all", [P, 1])
            inv = tmp("inv", [P, 1])
            top_ready = sem("top_ready")
            top_spread = sem("top_spread")
            shifted = sem("shifted")
            exp_ready = sem("exp_ready")
            sum_chain = sem("sum_chain")
            sum_spread = sem("sum_spread")
            NF = FULL * PER

            with nc.Block() as block:
                @block.gpsimd
                def _(pool):
                    pool.wait_ge(top_ready, 1)
                    nc.gpsimd.partition_all_reduce(top_all[:], top[:], P, RMAX).then_inc(top_spread, 1)
                    pool.wait_ge(sum_chain, 3)
                    nc.gpsimd.partition_all_reduce(total_all[:], total[:], P, RADD).then_inc(sum_spread, 1)

                @block.scalar
                def _(act):
                    act.wait_ge(top_spread, 1)
                    nc.scalar.mul(shift[:], top_all[:], -1.0 / H).then_inc(shifted, 1)
                    act.wait_ge(shifted, 1)
                    nc.scalar.activation(weight[:, 0:NF], score[:, 0:NF], ACT.Exp, bias=shift[:, 0:1], scale=1.0 / H,
                                         accum_out=sums[:, 0:1]).then_inc(exp_ready, 1)
                    nc.scalar.activation(weight[:, NF:], score[:, NF:], ACT.Exp, bias=shift[:, 0:1],
                                         scale=1.0 / H).then_inc(exp_ready, 1)

                @block.vector
                def _(dve):
                    nc.vector.tensor_reduce(top[:], score[:], AX_X, ALU.max).then_inc(top_ready, 1)
                    dve.wait_ge(exp_ready, 2)
                    nc.vector.tensor_tensor(weight[:, NF:], weight[:, NF:], tail_mask[:], ALU.mult).then_inc(sum_chain, 1)
                    dve.wait_ge(sum_chain, 1)
                    nc.vector.tensor_reduce(sums[:, 1:2], weight[:, NF:], AX_X, ALU.add).then_inc(sum_chain, 1)
                    dve.wait_ge(sum_chain, 2)
                    nc.vector.tensor_tensor(total[:], sums[:, 0:1], sums[:, 1:2], ALU.add).then_inc(sum_chain, 1)
                    dve.wait_ge(sum_spread, 1)
                    nc.vector.reciprocal(inv[:], total_all[:]).then_inc(sum_chain, 1)
                    dve.wait_ge(sum_chain, 4)
                    nc.vector.tensor_scalar(weight[:], weight[:], inv[:, 0:1], None, ALU.mult).then_inc(sum_chain, 1)

        with ExitStack() as st:
            def tmp(name, shape, dt=F32):
                return st.enter_context(nc.sbuf_tensor(name, shape, dt))

            def psum(name, shape):
                return st.enter_context(nc.psum_tensor(name, shape, F32))

            def sem(name):
                return st.enter_context(nc.semaphore(name))

            src_j = tmp("src_j", [P, UNROLL, PER], I32)
            dst_j = tmp("dst_j", [P, UNROLL, PER], I32)
            src_f = tmp("src_f", [P, UNROLL, PER])
            w_now = tmp("w_now", [P, UNROLL, PER])
            rel_j = tmp("rel_j", [P, 2, PER], BF16)
            one_j = tmp("one_j", [P, 2, PER, P])
            v_rows = tmp("v_rows", [P, UNROLL, PER, D])
            v_win = tmp("v_win", [P, UNROLL, D])
            w_rows = tmp("w_rows", [P, 2, PER, D])
            same = tmp("same", [P, 2, PER, P])
            same_b = tmp("same_b", [P, PER, P])
            before = tmp("before", [P, UNROLL, PER])
            dup = tmp("dup", [P, UNROLL, PER])
            move = tmp("move", [P, UNROLL, PER])
            row_i = tmp("row_i", [P, UNROLL, PER], I32)
            summed = tmp("summed", [P, UNROLL, PER, D])
            ps_r = psum("ps_r", [P, PER, P])
            ps_src = psum("ps_src", [P, PER, P])
            ps_v = psum("ps_v", [P, PER, P])
            ps_x = psum("ps_x", [P, PER, P])

            src_in = [sem(f"srcj_in{u}") for u in range(UNROLL)]
            dst_in = [sem(f"dstj_in{u}") for u in range(UNROLL)]
            v_in = [sem(f"v_in{u}") for u in range(UNROLL)]
            prep = sem("prep")
            rel_ready = sem("relj_ready")
            src_spread = sem("src_spread")
            counted = sem("counted")
            rel_spread = sem("relj_spread")
            one_ready = sem("onej_ready")
            same_ready = sem("same_ready")
            row_chain = sem("row_chain")
            v_made = sem("v_made")
            weighed = sem("weighed")
            x_made = sem("x_made")
            x_copied = sem("x_copied")
            added = [sem(f"added{r}") for r in range(COPIES)]
            AC = PER // COPIES
            J0, J1 = L0, L1
            A0 = UNROLL + 1
            A1_ = A0 + UNROLL * ((NG - 2 - A0) // UNROLL) - 1
            JLAST = NG

            with nc.Block() as block:
                @block.sync
                def _(sp):
                    def load(s, u, window):
                        e0 = group_edges(s)
                        if at_least(s, UNROLL):
                            sp.wait_ge(prep, s * 2 - (2 * UNROLL - 2))
                            sp.sem_inc(passed, 1)
                        sp.dma_start(src_j[:, u, :], src[bass.ds(e0, GE)].rearrange("(p j) -> p j", p=P)
                                     ).then_inc(src_in[u], 16)
                        if at_least(s, UNROLL):
                            if window:
                                sp.wait_ge(rel_ready, s - (UNROLL - 1))
                            else:
                                sp.wait_ge(v_in[u], count(s, u, 16 * PER, -UNROLL))
                            sp.sem_inc(passed, 1)
                        sp.dma_start(dst_j[:, u, :], dst[bass.ds(e0, GE)].rearrange("(p j) -> p j", p=P)
                                     ).then_inc(dst_in[u], 16)
                        if window:
                            if at_least(s, UNROLL):
                                sp.wait_ge(v_made, s * 2 - (2 * UNROLL - 2))
                            sp.sem_inc(passed, 1)
                            row = sp.value_load(base_i[0:1, bass.ds(s, 1)], min_val=0, max_val=N - P)
                            sp.dma_start(v_win[:, u, :], v_tab[bass.ds(row, P), :]).then_inc(v_in[u], 16)

                    branches(sp, lambda: run_steps(sp, 0, UNROLL, UNROLL * (LAST // UNROLL) - 1, LAST, lambda s, u: load(s, u, True)),
                             lambda: run_steps(sp, 0, UNROLL, UNROLL * (LAST // UNROLL) - 1, LAST, lambda s, u: load(s, u, False)))

                @block.gpsimd
                def _(pool):
                    def gather(s, u):
                        pool.wait_ge(dst_in[u], count(s, u, 16))
                        if at_least(s, UNROLL):
                            pool.wait_ge(weighed, s * 2 - (2 * UNROLL - 2))
                        pool.sem_inc(passed, 1)
                        for j in range(PER):
                            pool.indirect_dma_start(v_rows[:, u, j, :], None, v_tab,
                                                    bass.IndirectOffsetOnAxis(dst_j[:, u, j:j + 1], 0)
                                                    ).then_inc(v_in[u], 16)

                    def scatter(s, u):
                        pool.wait_ge(row_chain, s * 3 + 3)
                        for j in range(PER):
                            if j % HALF == 0:
                                pool.wait_ge(x_copied, s * 2 + (j // HALF + 1))
                            r, k = j % COPIES, j // COPIES
                            if at_least(s, 1) or k:
                                pool.wait_ge(added[r], s * (16 * AC) + 16 * k)
                            pool.sem_inc(passed, 1)
                            pool.indirect_dma_start(acc[r], bass.IndirectOffsetOnAxis(row_i[:, u, j:j + 1], 0),
                                                    summed[:, u, j, :], None, compute_op=ALU.add
                                                    ).then_inc(added[r], 16)

                    def step(s, u):
                        if in_group(s, 1):
                            gather(s + 1, (u + 1) % UNROLL)
                        if at_least(s, 1):
                            scatter(s - 1, (u - 1) % UNROLL)

                    def with_window():
                        run_steps(pool, 0, UNROLL, UNROLL * (LAST // UNROLL) - 1, LAST, scatter)

                    def with_gather():
                        gather(0, 0)
                        run_steps(pool, 0, J0, J1, JLAST, step)

                    branches(pool, with_window, with_gather)
                    for r in range(COPIES):
                        pool.wait_ge(added[r], 16 * AC * NG)

                @block.tensor
                def _(pe):
                    def spread_rel(s, u):
                        pe.wait_ge(rel_ready, s + 1)
                        for b in range(2):
                            if at_least(s, 1):
                                pe.wait_ge(one_ready, s * 2 - (1 - b))
                            for j in range(HALF * b, HALF * (b + 1)):
                                last = pe.matmul(ps_r[:, j, :], rel_j[:, u % 2, j:j + 1].to_broadcast([P, P]), ident_b[:],
                                                 start=True, stop=True)
                            last.then_inc(rel_spread, 1)

                    def spread_src(s, u):
                        pe.wait_ge(prep, s * 2 + 2)
                        for b in range(2):
                            if at_least(s, 1):
                                pe.wait_ge(counted, s * 2 - (1 - b))
                            for j in range(HALF * b, HALF * (b + 1)):
                                last = pe.matmul(ps_src[:, j, :], src_f[:, u, j:j + 1].to_broadcast([P, P]), ident[:],
                                                 start=True, stop=True)
                            last.then_inc(src_spread, 1)

                    def values(s, u):
                        pe.wait_ge(one_ready, s * 2 + 2)
                        pe.wait_ge(v_in[u], count(s, u, 16))
                        for b in range(2):
                            if at_least(s, 1):
                                pe.wait_ge(weighed, s * 2 - (1 - b))
                            for j in range(HALF * b, HALF * (b + 1)):
                                last = pe.matmul(ps_v[:, j, :], one_j[:, u % 2, j, :], v_win[:, u, :], start=True, stop=True)
                            last.then_inc(v_made, 1)

                    def combine(s, u):
                        for b in range(2):
                            pe.wait_ge(same_ready, s * 2 + (b + 1))
                            pe.wait_ge(weighed, s * 2 + (b + 1))
                            if at_least(s, 1):
                                pe.wait_ge(x_copied, s * 2 - (1 - b))
                            for j in range(HALF * b, HALF * (b + 1)):
                                last = pe.matmul(ps_x[:, j, :], same[:, u % 2, j, :], w_rows[:, u % 2, j, :], start=True,
                                                 stop=True)
                            last.then_inc(x_made, 1)

                    def step(s, u, window):
                        if window and in_group(s, 0):
                            values(s, u)
                        if window and in_group(s, 1):
                            spread_rel(s + 1, (u + 1) % UNROLL)
                        if at_least(s, 1):
                            combine(s - 1, (u - 1) % UNROLL)
                        if in_group(s, 1):
                            spread_src(s + 1, (u + 1) % UNROLL)

                    def path(window):
                        if window:
                            spread_rel(0, 0)
                        spread_src(0, 0)
                        run_steps(pe, 0, J0, J1, JLAST, lambda s, u: step(s, u, window))

                    branches(pe, lambda: path(True), lambda: path(False))

                @block.scalar
                def _(act):
                    def prepare(s, u, window):
                        act.wait_ge(src_in[u], count(s, u, 16))
                        if at_least(s, UNROLL):
                            act.wait_ge(row_chain, s * 3 - (3 * UNROLL - 3))
                            act.wait_ge(src_spread, s * 2 - (2 * UNROLL - 2))
                        nc.scalar.activation(src_f[:, u, :], src_j[:, u, :], ACT.Copy).then_inc(prep, 1)
                        nc.scalar.activation(w_now[:, u, :], weight[:, bass.ds(s * PER, PER)], ACT.Copy).then_inc(prep, 1)
                        if window:
                            act.wait_ge(dst_in[u], count(s, u, 16))
                            if at_least(s, 2):
                                act.wait_ge(rel_spread, s * 2 - 2)
                            nc.scalar.activation(rel_j[:, u % 2, :], dst_j[:, u, :], ACT.Identity,
                                                 bias=base_neg[:, bass.ds(s, 1)]).then_inc(rel_ready, 1)

                    def weigh(s, u, window):
                        act.wait_ge(prep, s * 2 + 2)
                        if not window:
                            act.wait_ge(v_in[u], count(s, u, 16 * PER))
                        for b in range(2):
                            if window:
                                act.wait_ge(v_made, s * 2 + (b + 1))
                            if at_least(s, 2):
                                act.wait_ge(x_made, s * 2 - (3 - b))
                            for j in range(HALF * b, HALF * (b + 1)):
                                op = nc.scalar.activation(w_rows[:, u % 2, j, :], ps_v[:, j, :] if window else v_rows[:, u, j, :],
                                                          ACT.Copy, scale=w_now[:, u, j:j + 1])
                            op.then_inc(weighed, 1)

                    def copy_sums(s, u):
                        for b in range(2):
                            act.wait_ge(x_made, s * 2 + (b + 1))
                            if b == 0 and at_least(s, UNROLL):
                                for r in range(COPIES):
                                    act.wait_ge(added[r], s * (16 * AC) - 16 * AC * (UNROLL - 1))
                            h0, h1 = HALF * b, HALF * (b + 1)
                            nc.scalar.activation(summed[:, u, h0:h1, :], ps_x[:, h0:h1, :], ACT.Copy).then_inc(x_copied, 1)

                    def step(s, u, window):
                        if in_group(s, 2):
                            prepare(s + 2, (u + 2) % UNROLL, window)
                        if in_group(s, 0):
                            weigh(s, u, window)
                        if at_least(s, 1):
                            copy_sums(s - 1, (u - 1) % UNROLL)

                    def path(window):
                        prepare(0, 0, window)
                        prepare(1, 1, window)
                        run_steps(act, 0, A0, A1_, JLAST, lambda s, u: step(s, u, window))

                    branches(act, lambda: path(True), lambda: path(False))

                @block.vector
                def _(dve):
                    def one_hot(s, u):
                        for b in range(2):
                            dve.wait_ge(rel_spread, s * 2 + (b + 1))
                            if b == 0 and at_least(s, 2):
                                dve.wait_ge(v_made, s * 2 - 2)
                            h0, h1 = HALF * b, HALF * (b + 1)
                            nc.vector.tensor_scalar(one_j[:, u % 2, h0:h1, :], ps_r[:, h0:h1, :], part[:, 0:1], None,
                                                    ALU.is_equal).then_inc(one_ready, 1)

                    def compare(s, u):
                        for b in range(2):
                            dve.wait_ge(src_spread, s * 2 + (b + 1))
                            if b == 0:
                                if at_least(s, 2):
                                    dve.wait_ge(x_made, s * 2 - 2)
                            h0, h1 = HALF * b, HALF * (b + 1)
                            nc.vector.tensor_tensor(same[:, u % 2, h0:h1, :], ps_src[:, h0:h1, :],
                                                    src_f[:, u, h0:h1].rearrange("p (j a) -> p j a", a=1).to_broadcast([P, HALF, P]),
                                                    ALU.is_equal).then_inc(same_ready, 1)
                            for j in range(h0, h1):
                                op = nc.vector.scalar_tensor_tensor(same_b[:, j, :], ps_src[:, j, :], src_f[:, u, j:j + 1],
                                                                    earlier[:], ALU.is_equal, ALU.mult,
                                                                    accum_out=before[:, u, j:j + 1])
                            op.then_inc(counted, 1)
                        if at_least(s, UNROLL):
                            for r in range(COPIES):
                                dve.wait_ge(added[r], s * (16 * AC) - 16 * AC * (UNROLL - 1))
                        dve.wait_ge(counted, s * 2 + 2)
                        nc.vector.tensor_scalar(dup[:, u, :], before[:, u, :], 1.0, None, ALU.min).then_inc(row_chain, 1)
                        dve.wait_ge(row_chain, s * 3 + 1)
                        nc.vector.scalar_tensor_tensor(move[:, u, :], src_f[:, u, :], part[:, 1:2], dup[:, u, :],
                                                       ALU.subtract, ALU.mult).then_inc(row_chain, 1)
                        dve.wait_ge(row_chain, s * 3 + 2)
                        nc.vector.tensor_tensor(row_i[:, u, :], src_f[:, u, :], move[:, u, :],
                                                ALU.subtract).then_inc(row_chain, 1)

                    def step(s, u, window):
                        if in_group(s, 1):
                            if window:
                                one_hot(s + 1, (u + 1) % UNROLL)
                            compare(s + 1, (u + 1) % UNROLL)

                    def path(window):
                        if window:
                            one_hot(0, 0)
                        compare(0, 0)
                        run_steps(dve, 0, J0, J1, LAST, lambda s, u: step(s, u, window))

                    branches(dve, lambda: path(True), lambda: path(False))

        with ExitStack() as st:
            def tmp(name, shape, dt=F32):
                return st.enter_context(nc.sbuf_tensor(name, shape, dt))

            def sem(name):
                return st.enter_context(nc.semaphore(name))

            sums_in = tmp("sums_in", [P, UNROLL, COPIES, NB, D])
            y_stats = tmp("y_stats", [P, 2, NB, 6])
            y_mv = tmp("y_mv", [P, 2, NB, 2])
            y_std = tmp("y_std", [P, 2, NB])
            y_rstd = tmp("y_rstd", [P, 2, NB])
            y_g = tmp("y_g", [P, 2, NB, D])
            o_sb = tmp("o_sb", [P, 2, NB, D])
            ps_y = st.enter_context(nc.psum_tensor("ps_y", [P, 2, NB, D], F32))

            acc_in = [sem(f"acc_in{u}") for u in range(UNROLL)]
            pair_added = sem("pair_added")
            y_ready = sem("y_ready")
            y_chain = sem("y_chain")
            y_std_ready = sem("y_std_ready")
            y_rstd_ready = sem("y_rstd_ready")
            y_g_ready = sem("y_g_ready")
            x_beta = sem("x_beta")
            o_ready = sem("o_ready")
            o_out = [sem("o_out0"), sem("o_out1")]

            def n_tiles(s):
                return 2 if known(s) and s == NSTEP else NB

            def final_steps(eng, step):
                run_steps(eng, 0, UNROLL, NSTEP - 1, NSTEP + 1, step)

            def upto(s, n):
                return (not known(s)) or s <= n

            with nc.Block() as block:
                @block.sync
                def _(sp):
                    def load(s, u):
                        if at_least(s, UNROLL):
                            sp.wait_ge(y_ready, s - (UNROLL - 1))
                        for r in range(COPIES):
                            if known(s) and s == NSTEP:
                                sp.dma_start(sums_in[:, u, r, 0:1, :], nodes_of(acc[r], s * NB, 1)).then_inc(acc_in[u], 16)
                                sp.dma_start(sums_in[0:NREM, u, r, 1, :], nodes_of(acc[r], TR, 1)).then_inc(acc_in[u], 16)
                            else:
                                sp.dma_start(sums_in[:, u, r, :, :], nodes_of(acc[r], s * NB, NB)).then_inc(acc_in[u], 16)

                    final_steps(sp, lambda s, u: load(s, u) if upto(s, NSTEP) else None)

                @block.gpsimd
                def _(pool):
                    def step(s, u):
                        if not upto(s, NSTEP):
                            return
                        n = n_tiles(s)
                        if known(s) and s == NSTEP:
                            pool.wait_ge(acc_in[u], count(s, u, 16 * COPIES) + 16 * COPIES)
                        else:
                            pool.wait_ge(acc_in[u], count(s, u, 16 * COPIES))
                        a, b = (sums_in[:, u, COPIES - k, 0:n, :] for k in (2, 1))
                        nc.gpsimd.tensor_tensor(a, a, b, ALU.add).then_inc(pair_added, 1)
                        for k in range(n):
                            xt = x_sb[:, bass.ds(s * NB + k, 1), :].rearrange("p a k -> p (a k)")
                            op = nc.gpsimd.tensor_tensor(xt, xt, beta_b[:], ALU.add)
                        op.then_inc(x_beta, 1)

                    final_steps(pool, step)

                @block.tensor
                def _(pe):
                    def add_up(s, u):
                        pe.wait_ge(pair_added, s + 1)
                        if at_least(s, 2):
                            pe.wait_ge(y_g_ready, (s - 1) * NB)
                        n = n_tiles(s)
                        y = ps_y[:, u % 2, 0:n, :]
                        pe.matmul(y, ident[:], h_sb[:, bass.ds(s * NB, n), :], start=True, stop=False)
                        for r in range(COPIES - 1):
                            last = pe.matmul(y, ident[:], sums_in[:, u, r, 0:n, :], start=False, stop=(r == COPIES - 2))
                        last.then_inc(y_ready, 1)

                    final_steps(pe, lambda s, u: add_up(s, u) if upto(s, NSTEP) else None)

                @block.scalar
                def _(act):
                    def root(s, u):
                        act.wait_ge(y_chain, (s + 1) * 2)
                        if at_least(s, 2):
                            act.wait_ge(y_rstd_ready, s - 1)
                        nc.scalar.activation(y_std[:, u % 2, :], y_mv[:, u % 2, :, 1], ACT.Sqrt, bias=eps[:, 0:1]
                                             ).then_inc(y_std_ready, 1)

                    def store(s, u):
                        act.wait_ge(o_ready, (s + 1) * NB if n_tiles(s) == NB else NSTEP * NB + 2)
                        if known(s) and s == NSTEP:
                            act.dma_start(nodes_of(out, s * NB, 1), o_sb[:, u % 2, 0:1, :]).then_inc(o_out[u % 2], 16)
                            act.dma_start(nodes_of(out, TR, 1), o_sb[0:NREM, u % 2, 1, :]).then_inc(o_out[u % 2], 16)
                        else:
                            act.dma_start(nodes_of(out, s * NB, NB), o_sb[:, u % 2, :, :]).then_inc(o_out[u % 2], 16)

                    def step(s, u):
                        if upto(s, NSTEP):
                            root(s, u)
                        if at_least(s, 1):
                            store(s - 1, u + 1)

                    final_steps(act, step)
                    act.wait_ge(o_out[0], 16 * (NSTEP // 2) + 32)
                    act.wait_ge(o_out[1], 16 * (NSTEP // 2))

                @block.vector
                def _(dve):
                    def measure(s, u):
                        dve.wait_ge(y_ready, s + 1)
                        n = n_tiles(s)
                        for k in range(n):
                            op = nc.vector.bn_stats(y_stats[:, u % 2, k, :], ps_y[:, u % 2, k, :])
                        op.then_inc(y_chain, 1)
                        dve.wait_ge(y_chain, s * 2 + 1)
                        if at_least(s, 2):
                            dve.wait_ge(y_std_ready, s - 1)
                        dve.sem_inc(passed, 1)
                        for k in range(NB):
                            op = nc.vector.bn_aggr(y_mv[:, u % 2, k, :], y_stats[:, u % 2, k, :])
                        op.then_inc(y_chain, 1)

                    def finish(s, u):
                        dve.wait_ge(y_std_ready, s + 1)
                        nc.vector.reciprocal(y_rstd[:, u % 2, :], y_std[:, u % 2, :]).then_inc(y_rstd_ready, 1)
                        n = n_tiles(s)
                        for k in range(n):
                            nc.vector.scalar_tensor_tensor(y_g[:, u % 2, k, :], ps_y[:, u % 2, k, :], y_mv[:, u % 2, k, 0:1], gamma_b[:],
                                                           ALU.subtract, ALU.mult).then_inc(y_g_ready, 1)
                        dve.wait_ge(y_rstd_ready, s + 1)
                        dve.wait_ge(x_beta, s + 1)
                        if at_least(s, 2):
                            dve.wait_ge(o_out[u % 2], s * 8 - u % 2 * 8)
                        for k in range(n):
                            dve.wait_ge(y_g_ready, s * NB + (k + 1))
                            nc.vector.scalar_tensor_tensor(o_sb[:, u % 2, k, :], y_g[:, u % 2, k, :], y_rstd[:, u % 2, k:k + 1],
                                                           x_sb[:, bass.ds(s * NB + k, 1), :].rearrange("p a k -> p (a k)"),
                                                           ALU.mult, ALU.add).then_inc(o_ready, 1)

                    def step(s, u):
                        if upto(s, NSTEP):
                            measure(s, u)
                        if at_least(s, 1):
                            finish(s - 1, u + 1)

                    final_steps(dve, step)


NAMES = ["x", "src", "dst", "edge_attr_64"] + ["L0_gnn_" + n for n in (
    "Wn", "bn", "Wq", "bq", "Wk", "bk", "Wv", "bv", "We", "be", "A1", "b1", "A2", "b2", "gamma", "beta")]


def kernel(**inputs):
    import numpy as np
    import concourse.bacc as bacc
    from concourse.bass_utils import run_bass_kernel_spmd

    nc = bacc.Bacc("TRN2", target_bir_lowering=False, num_devices=1)
    arrays, args = {}, []
    for name in NAMES:
        a = np.ascontiguousarray(inputs[name])
        arrays[name + "_dram"] = a
        args.append(nc.dram_tensor(name + "_dram", a.shape, mybir.dt.from_np(a.dtype), kind="ExternalInput").ap())
    shape = arrays["x_dram"].shape
    args.append(nc.dram_tensor("out_dram", shape, F32, kind="ExternalOutput").ap())
    gnn_layer(nc, *args)
    r = run_bass_kernel_spmd(nc, [arrays], core_ids=[0])
    return r.results[0]["out_dram"]
```

```python
from contextlib import ExitStack

import concourse.bass as bass
from concourse import mybir

P = 128
PER = 8
GE = P * PER
UNROLL = 4
COPIES = 4
HALF = PER // 2
EPS = 1e-5
SLOPE = 0.2

ALU = mybir.AluOpType
ACT = mybir.ActivationFunctionType
F32 = mybir.dt.float32
BF16 = mybir.dt.bfloat16
I32 = mybir.dt.int32
AX_X = mybir.AxisListType.X
RMAX = bass.bass_isa.ReduceOp.max
RADD = bass.bass_isa.ReduceOp.add


def run_steps(eng, first, loop_from, loop_to, last, step):
    assert (loop_to + 1 - loop_from) % UNROLL == 0
    for s in range(first, loop_from):
        step(s, s % UNROLL)
    with eng.Fori(0, (loop_to + 1 - loop_from) // UNROLL) as i:
        for k in range(UNROLL):
            step(i * UNROLL + (loop_from + k), (loop_from + k) % UNROLL)
    for s in range(loop_to + 1, last + 1):
        step(s, s % UNROLL)


def known(s):
    return isinstance(s, int)


def at_least(s, n):
    return (not known(s)) or s >= n


def count(s, u, unit, ahead=0):
    g, v = s + ahead, (u + ahead) % UNROLL
    if known(s):
        return unit * (g // UNROLL + 1)
    return (g - v) * (unit // UNROLL) + unit


def gnn_layer(nc, x, src, dst, edge, Wn, bn, Wq, bq, Wk, bk, Wv, bv, We, be, A1, b1, A2, b2,
              gamma, beta, out):
    N, D = x.shape
    E, DE = edge.shape
    H = A2.shape[1]
    assert D == P and DE == P // 2
    FULL = E // GE
    LAST = FULL
    NG = FULL + 1
    TAIL0 = E - GE
    AGAIN = FULL * GE - TAIL0
    TR = N // P
    NREM = N - TR * P
    NT = TR + 1
    ROWS = -(-(N + P) // P) * P
    CH = -(-NG // P)
    assert E % GE and N % P

    q_tab = nc.dram_tensor("q_tab", [N, D], F32).ap()
    k_tab = nc.dram_tensor("k_tab", [N, D], F32).ap()
    v_tab = nc.dram_tensor("v_tab", [N, D], F32).ap()
    acc = [nc.dram_tensor(f"acc{r}", [ROWS, D], F32).ap() for r in range(COPIES)]

    def nodes_of(table, t, n, w=D):
        if known(t) and t == TR:
            return table[TR * P:N, :]
        return table[0:TR * P, :].rearrange("(p t) f -> p t f", t=TR)[:, bass.ds(t, n), :]

    with ExitStack() as ctx:
        def sb(name, shape, dt=F32):
            return ctx.enter_context(nc.sbuf_tensor(name, shape, dt))

        passed = ctx.enter_context(nc.semaphore("passed"))

        zeros = sb("zeros", [P, D])
        eps = sb("eps", [P, 1])
        ident = sb("ident", [P, P])
        ident_b = sb("ident_b", [P, P], BF16)
        earlier = sb("earlier", [P, P])
        part_i = sb("part_i", [P, 2], I32)
        part = sb("part", [P, 2])
        tail_mask = sb("tail_mask", [P, PER])
        x_sb = sb("x_sb", [P, NT, D])
        h_sb = sb("h_sb", [P, NT, D])
        w2 = sb("w2", [P, D])
        a2 = sb("a2", [P, H])
        b2_rep = sb("b2_rep", [P, PER, H])
        gamma_b = sb("gamma_b", [P, D])
        beta_b = sb("beta_b", [P, D])
        base_neg = sb("base_neg", [P, CH * P])
        base_i = sb("base_i", [P, CH * P], I32)
        local_i = sb("local_i", [P, 1], I32)
        score = sb("score", [P, NG * PER])
        weight = sb("weight", [P, NG * PER])
        top_of = sb("top_of", [P, 2])
        total_all = sb("total_all", [P, 1])

        NB = 4
        NSTEP = TR // NB
        assert TR % NB == 1
        with ExitStack() as st:
            def tmp(name, shape, dt=F32):
                return st.enter_context(nc.sbuf_tensor(name, shape, dt))

            def psum(name, shape):
                return st.enter_context(nc.psum_tensor(name, shape, F32))

            def sem(name):
                return st.enter_context(nc.semaphore(name))

            wm = tmp("wm", [P, 4 * D])
            bias = tmp("bias", [P, 4 * D])
            wq = tmp("wq", [P, D])
            wk = tmp("wk", [P, D])
            we = tmp("we", [DE, D])
            a1 = tmp("a1", [P, 3, D])
            bcol = tmp("bcol", [P, 3])
            b2_b = tmp("b2_b", [P, H])
            wqT = tmp("wqT", [P, D])
            wkT = tmp("wkT", [P, D])
            weT = tmp("weT", [P, 2, DE])
            stats = tmp("stats", [P, UNROLL, NB, 6])
            mv = tmp("mv", [P, UNROLL, NB, 2])
            std = tmp("std", [P, NT])
            rstd = tmp("rstd", [P, NT])
            shift_x = tmp("shift_x", [P, NT])
            xn = tmp("xn", [P, 2, NB, D])
            hT = tmp("hT", [P, 2, NB * P])
            tabs = tmp("tabs", [P, 2, 3, NB, D])
            raw = tmp("raw", [P, 2, 4 * D])
            dgroup = tmp("dgroup", [P, CH, GE], I32)
            dmin = tmp("dmin", [P, CH])
            dmax = tmp("dmax", [P, CH])
            dspan = tmp("dspan", [P, CH])
            span = tmp("span", [P, 1])
            ps_t = psum("ps_t", [P, 2, 512])
            ps_m = psum("ps_m", [P, NB, 512])
            ps_w = psum("ps_w", [P, 2, 512])

            made = sem("made")
            w_in = sem("w_in")
            more_in = sem("more_in")
            x_in = [sem(f"x_in{u}") for u in range(UNROLL)]
            d_in = sem("d_in")
            w_turned = sem("w_turned")
            w_copied = sem("w_copied")
            w_made = sem("w_made")
            ready = sem("ready")
            stat_chain = sem("stat_chain")
            std_ready = sem("std_ready")
            scale_chain = sem("scale_chain")
            xn_ready = sem("xn_ready")
            turned = sem("turned")
            hT_ready = sem("hT_ready")
            m_ready = sem("m_ready")
            tab_ready = sem("tab_ready")
            raw_ready = sem("raw_ready")
            pool_tab_ready = sem("pool_tab_ready")
            x_beta = sem("x_beta")
            span_found = sem("span_found")
            stored = [sem("stored0"), sem("stored1")]
            span_chain = sem("span_chain")
            span_turned = sem("span_turned")

            N_MADE = 12
            ON_DVE = NB - 1
            LOADS = 16
            FIRST_LOADS = 7
            LOOP_END = 16
            assert NSTEP - LOOP_END >= 2 * CH

            def tiles(s):
                return 2 if known(s) and s == NSTEP else NB

            def upto_last(s):
                return (not known(s)) or 0 <= s <= NSTEP

            def node_steps(eng, step):
                run_steps(eng, -3, UNROLL + 1, LOOP_END, NSTEP, step)

            with nc.Block() as block:
                @block.gpsimd
                def _(pool):
                    nc.gpsimd.memset(x_sb[:, TR, :], 0.0).then_inc(made, 1)
                    nc.gpsimd.memset(dgroup[:, CH - 1, :], 0).then_inc(made, 1)
                    nc.gpsimd.memset(eps[:], EPS).then_inc(made, 1)
                    nc.gpsimd.memset(ident[:], 0.0).then_inc(made, 1)
                    nc.gpsimd.memset(earlier[:], 1.0).then_inc(made, 1)
                    nc.gpsimd.memset(tail_mask[:], 1.0).then_inc(made, 1)
                    nc.gpsimd.memset(zeros[:], 0.0).then_inc(made, 1)
                    pool.wait_ge(made, 7)
                    nc.gpsimd.affine_select(out=ident[:], in_=ident[:], compare_op=ALU.not_equal, fill=1.0,
                                            base=0, pattern=[[-1, P]], channel_multiplier=1).then_inc(made, 1)
                    nc.gpsimd.affine_select(out=earlier[:], in_=earlier[:], compare_op=ALU.is_gt, fill=0.0,
                                            base=0, pattern=[[-1, P]], channel_multiplier=1).then_inc(made, 1)
                    nc.gpsimd.affine_select(out=tail_mask[:], in_=tail_mask[:], compare_op=ALU.is_ge, fill=0.0,
                                            base=-AGAIN, pattern=[[1, PER]], channel_multiplier=PER).then_inc(made, 1)
                    nc.gpsimd.iota(part_i[:, 0:1], [[0, 1]], base=0, channel_multiplier=1).then_inc(made, 1)
                    nc.gpsimd.iota(part_i[:, 1:2], [[0, 1]], base=N, channel_multiplier=1).then_inc(made, 1)

                    def add_beta(s):
                        pool.wait_ge(xn_ready, s + 1)
                        n = tiles(s)
                        xt = x_sb[:, bass.ds(s * NB, n), :]
                        nc.gpsimd.tensor_tensor(xt, xt, beta_b[:].rearrange("p (a f) -> p a f", a=1).to_broadcast([P, n, D]),
                                                ALU.add).then_inc(x_beta, 1)

                    def add_bias(s, u):
                        pool.wait_ge(raw_ready, s + 1)
                        nc.gpsimd.tensor_tensor(h_sb[:, bass.ds(s * NB + (NB - 1), 1), :].rearrange("p a k -> p (a k)"),
                                                raw[:, u % 2, 0:D], bias[:, 0:D], ALU.add).then_inc(pool_tab_ready, 1)
                        if at_least(s, 2):
                            pool.wait_ge(stored[u % 2], (s - u % 2) * 24)
                        nc.gpsimd.tensor_tensor(tabs[:, u % 2, :, NB - 1, :],
                                                raw[:, u % 2, D:4 * D].rearrange("p (a f) -> p a f", a=3),
                                                bias[:, D:4 * D].rearrange("p (a f) -> p a f", a=3),
                                                ALU.add).then_inc(pool_tab_ready, 1)

                    def step(s, u):
                        if upto_last(s):
                            add_beta(s)
                        if upto_last(s) and tiles(s) == NB:
                            add_bias(s, u)

                    pool.wait_ge(more_in, 16 * (LOADS - FIRST_LOADS))
                    pool.wait_ge(ready, 6 + PER)
                    node_steps(pool, step)

                @block.sync
                def _(sp):
                    row = lambda v: v.rearrange("(a d) -> a d", a=1).to_broadcast([P, v.shape[0]])
                    col = lambda v: v.rearrange("(d a) -> d a", a=1)

                    def load_x(s, u):
                        if known(s) and s == NSTEP:
                            sp.wait_ge(made, 7)
                            sp.dma_start(x_sb[:, s * NB:s * NB + 1, :], nodes_of(x, s * NB, 1)).then_inc(x_in[u], 16)
                            sp.dma_start(x_sb[0:NREM, TR, :], nodes_of(x, TR, 1)).then_inc(x_in[u], 16)
                        else:
                            sp.dma_start(x_sb[:, bass.ds(s * NB, NB), :], nodes_of(x, s * NB, NB)).then_inc(x_in[u], 16)

                    loads = [
                        (wq[:], Wq), (wk[:], Wk), (we[:], We),
                        (a1[:], A1.rearrange("(c p) f -> p c f", p=P)),
                        (bcol[:, 0:1], col(bq)), (bcol[:, 1:2], col(bk)), (bcol[:, 2:3], col(be)),
                        (wm[:, 0:D], Wn), (wm[:, 3 * D:4 * D], Wv), (a2[:], A2),
                        (bias[:, 0:D], row(bn)), (bias[:, 2 * D:3 * D], row(b1)), (bias[:, 3 * D:4 * D], row(bv)),
                        (b2_b[:], row(b2)), (gamma_b[:], row(gamma)), (beta_b[:], row(beta)),
                    ]
                    assert len(loads) == LOADS
                    load_x(0, 0)
                    for d, s in loads[:FIRST_LOADS]:
                        sp.dma_start(d, s).then_inc(w_in, 16)
                    load_x(1, 1)
                    for d, s in loads[FIRST_LOADS:]:
                        sp.dma_start(d, s).then_inc(more_in, 16)
                    load_x(2, 2)
                    load_x(3, 3)
                    for c in range(CH - 1):
                        sp.dma_start(dgroup[:, c, :], dst[c * P * GE:(c + 1) * P * GE].rearrange("(g e) -> g e", g=P)
                                     ).then_inc(d_in, 16)
                    sp.wait_ge(made, 7)
                    rest = FULL - (CH - 1) * P
                    sp.dma_start(dgroup[0:rest, CH - 1, :],
                                 dst[(CH - 1) * P * GE:FULL * GE].rearrange("(g e) -> g e", g=rest)).then_inc(d_in, 16)
                    sp.dma_start(dgroup[rest:rest + 1, CH - 1, :],
                                 dst[TAIL0:E].rearrange("(g e) -> g e", g=1)).then_inc(d_in, 16)

                    def step(s, u):
                        if upto_last(s + 3 + UNROLL):
                            sp.wait_ge(stat_chain, s * 2 + 7)
                            load_x(s + 3 + UNROLL, (u + 3) % UNROLL)
                        if known(s) and s < 0:
                            return
                        sp.wait_ge(tab_ready, s * (2 * ON_DVE) + 2 * min(tiles(s), ON_DVE))
                        if tiles(s) == NB:
                            sp.wait_ge(pool_tab_ready, (s + 1) * 2)
                        for i, table in enumerate((q_tab, k_tab, v_tab)):
                            if tiles(s) == NB:
                                sp.dma_start(nodes_of(table, s * NB, NB), tabs[:, u % 2, i, :, :]).then_inc(stored[u % 2], 16)
                            else:
                                sp.dma_start(nodes_of(table, s * NB, 1), tabs[:, u % 2, i, 0:1, :]).then_inc(stored[u % 2], 16)
                                sp.dma_start(nodes_of(table, TR, 1), tabs[0:NREM, u % 2, i, 1, :]).then_inc(stored[u % 2], 16)

                    node_steps(sp, step)
                    sp.wait_ge(stored[0], 48 * (NSTEP // 2) + 96)
                    sp.wait_ge(stored[1], 48 * (NSTEP // 2))

                @block.tensor
                def _(pe):
                    pe.wait_ge(made, N_MADE)
                    pe.wait_ge(w_in, 16 * FIRST_LOADS)
                    pe.transpose(ps_w[:, 0, 0:P], wq[:], ident[:])
                    pe.transpose(ps_w[:, 0, P:2 * P], wk[:], ident[:])
                    pe.transpose(ps_w[:, 0, 2 * P:2 * P + DE], we[:], ident[0:DE, 0:DE]).then_inc(w_turned, 1)
                    pe.wait_ge(w_copied, 4)
                    pe.matmul(ps_w[:, 1, 0:P], wqT[:], a1[:, 0, :], start=True, stop=True)
                    pe.matmul(ps_w[:, 1, P:2 * P], wkT[:], a1[:, 1, :], start=True, stop=True)
                    pe.matmul(ps_w[:, 1, 2 * P:3 * P], weT[:].rearrange("p a k -> p (a k)"), a1[:, 2, :],
                              start=True, stop=True)
                    pe.matmul(ps_w[:, 0, 0:P], bcol[:, 0:1].to_broadcast([P, P]), a1[:, 0, :], start=True, stop=True)
                    pe.matmul(ps_w[:, 0, P:2 * P], bcol[:, 1:2].to_broadcast([P, P]), a1[:, 1, :], start=True, stop=False)
                    pe.matmul(ps_w[:, 0, P:2 * P], bcol[:, 2:3].to_broadcast([P, P]), a1[:, 2, :], start=False,
                              stop=True).then_inc(w_made, 1)

                    def turn(s, u):
                        pe.wait_ge(xn_ready, s + 1)
                        if at_least(s, 2):
                            pe.wait_ge(hT_ready, s - 1)
                        for k in range(tiles(s)):
                            last = pe.transpose(ps_t[:, u % 2, k * P:(k + 1) * P], xn[:, u % 2, k, :], ident[:])
                        last.then_inc(turned, 1)

                    def project(s, u):
                        pe.wait_ge(hT_ready, s + 1)
                        if known(s) and s == 0:
                            pe.wait_ge(ready, 6 + PER)
                        for k in range(tiles(s)):
                            if at_least(s, 1) and k < ON_DVE:
                                pe.wait_ge(tab_ready, s * (2 * ON_DVE) - 2 * (ON_DVE - 1 - k))
                            elif at_least(s, 1):
                                pe.wait_ge(raw_ready, s)
                            pe.matmul(ps_m[:, k, :], hT[:, u % 2, k * P:(k + 1) * P], wm[:], start=True,
                                      stop=True).then_inc(m_ready, 1)

                    def step(s, u):
                        if upto_last(s + 1):
                            turn(s + 1, u + 1)
                        if upto_last(s):
                            project(s, u)

                    node_steps(pe, step)
                    pe.wait_ge(span_chain, 2)
                    for c in range(CH):
                        pe.matmul(ps_w[:, 0, c * P:(c + 1) * P], dmin[:, c:c + 1].to_broadcast([P, P]), ident[:],
                                  start=True, stop=True)
                        last = pe.matmul(ps_w[:, 1, c * P:(c + 1) * P], dspan[:, c:c + 1].to_broadcast([P, P]), ident[:],
                                         start=True, stop=True)
                    last.then_inc(span_turned, 1)

                @block.scalar
                def _(act):
                    act.wait_ge(made, 3)

                    def root(s, u):
                        act.wait_ge(stat_chain, s * 2 + 2)
                        t, n = s * NB, tiles(s)
                        nc.scalar.activation(std[:, bass.ds(t, n)], mv[:, u, 0:n, 1], ACT.Sqrt,
                                             bias=eps[:, 0:1]).then_inc(std_ready, 1)

                    def normal(s, u):
                        act.wait_ge(scale_chain, s * 2 + 2)
                        if at_least(s, 2):
                            act.wait_ge(turned, s - 1)
                        for k in range(tiles(s)):
                            t = s * NB + k
                            op = nc.scalar.activation(xn[:, u % 2, k, :], x_sb[:, bass.ds(t, 1), :].rearrange("p a k -> p (a k)"),
                                                      ACT.Identity, scale=rstd[:, bass.ds(t, 1)], bias=shift_x[:, bass.ds(t, 1)])
                        op.then_inc(xn_ready, 1)

                    def relu(s, u):
                        act.wait_ge(turned, s + 1)
                        if at_least(s, 2):
                            act.wait_ge(m_ready, (s - 1) * NB)
                        w = tiles(s) * P
                        nc.scalar.activation(hT[:, u % 2, 0:w], ps_t[:, u % 2, 0:w], ACT.Relu).then_inc(hT_ready, 1)

                    def copy_last(s, u):
                        act.wait_ge(m_ready, (s + 1) * NB)
                        if at_least(s, 2):
                            act.wait_ge(pool_tab_ready, (s - 1) * 2)
                        nc.scalar.activation(raw[:, u % 2, :], ps_m[:, NB - 1, :], ACT.Copy).then_inc(raw_ready, 1)

                    def step(s, u):
                        if upto_last(s + 1):
                            relu(s + 1, u + 1)
                        if upto_last(s + 2):
                            normal(s + 2, u)
                        if upto_last(s + 3):
                            root(s + 3, (u + 3) % UNROLL)
                        if upto_last(s) and tiles(s) == NB:
                            copy_last(s, u)

                    node_steps(act, step)

                @block.vector
                def _(dve):
                    def stats_of(s, u):
                        dve.wait_ge(x_in[u], count(s, u, 16) if tiles(s) == NB else count(s, u, 16) + 16)
                        for k in range(tiles(s)):
                            t = s * NB + k
                            op = nc.vector.bn_stats(stats[:, u, k, :], x_sb[:, bass.ds(t, 1), :].rearrange("p a k -> p (a k)"))
                        op.then_inc(stat_chain, 1)
                        dve.wait_ge(stat_chain, s * 2 + 1)
                        dve.sem_inc(passed, 1)
                        for k in range(tiles(s)):
                            t = s * NB + k
                            op = nc.vector.bn_aggr(mv[:, u, k, :], stats[:, u, k, :])
                        op.then_inc(stat_chain, 1)

                    def scale_of(s, u):
                        dve.wait_ge(std_ready, s + 1)
                        t, n = s * NB, tiles(s)
                        nc.vector.reciprocal(rstd[:, bass.ds(t, n)], std[:, bass.ds(t, n)]).then_inc(scale_chain, 1)
                        dve.wait_ge(scale_chain, s * 2 + 1)
                        nc.vector.scalar_tensor_tensor(shift_x[:, bass.ds(t, n)], mv[:, u, 0:n, 0], -1.0,
                                                       rstd[:, bass.ds(t, n)], ALU.mult, ALU.mult).then_inc(scale_chain, 1)

                    def add_bias(s, u):
                        if at_least(s, 2):
                            dve.wait_ge(stored[u % 2], (s - u % 2) * 24)
                        for k in range(min(tiles(s), ON_DVE)):
                            dve.wait_ge(m_ready, s * NB + (k + 1))
                            nc.vector.tensor_tensor(h_sb[:, bass.ds(s * NB + k, 1), :].rearrange("p a k -> p (a k)"),
                                                    ps_m[:, k, 0:D], bias[:, 0:D], ALU.add).then_inc(tab_ready, 1)
                            nc.vector.tensor_tensor(tabs[:, u % 2, :, k, :], ps_m[:, k, D:4 * D].rearrange("p (a f) -> p a f", a=3),
                                                    bias[:, D:4 * D].rearrange("p (a f) -> p a f", a=3),
                                                    ALU.add).then_inc(tab_ready, 1)

                    def turned_weights():
                        dve.wait_ge(w_turned, 1)
                        nc.vector.tensor_copy(wqT[:], ps_w[:, 0, 0:P]).then_inc(w_copied, 1)
                        nc.vector.tensor_copy(wkT[:], ps_w[:, 0, P:2 * P]).then_inc(w_copied, 1)
                        nc.vector.tensor_copy(weT[:, 0, :], ps_w[:, 0, 2 * P:2 * P + DE]).then_inc(w_copied, 1)
                        nc.vector.tensor_copy(weT[:, 1, :], ps_w[:, 0, 2 * P:2 * P + DE]).then_inc(w_copied, 1)

                    def weights_of():
                        dve.wait_ge(w_made, 1)
                        dve.wait_ge(more_in, 16 * (LOADS - FIRST_LOADS))
                        nc.vector.tensor_copy(wm[:, D:3 * D], ps_w[:, 1, 0:2 * D]).then_inc(ready, 1)
                        nc.vector.tensor_copy(w2[:], ps_w[:, 1, 2 * D:3 * D]).then_inc(ready, 1)
                        nc.vector.tensor_copy(bias[:, D:2 * D], ps_w[:, 0, 0:D]).then_inc(ready, 1)
                        nc.vector.tensor_tensor(bias[:, 2 * D:3 * D], bias[:, 2 * D:3 * D], ps_w[:, 0, D:2 * D],
                                                ALU.add).then_inc(ready, 1)
                        for j in range(PER):
                            nc.vector.tensor_copy(b2_rep[:, j, :], b2_b[:]).then_inc(ready, 1)
                        nc.vector.tensor_copy(part[:], part_i[:]).then_inc(ready, 1)
                        nc.vector.tensor_copy(ident_b[:], ident[:]).then_inc(ready, 1)
                        dve.wait_ge(ready, 6 + PER)

                    def reach(i):
                        if i == 0:
                            dve.wait_ge(d_in, 16 * (CH + 1))
                        end, op = ((dmin, ALU.min), (dmax, ALU.max))[i % 2]
                        nc.vector.tensor_reduce(end[:, i // 2:i // 2 + 1], dgroup[:, i // 2, :], AX_X, op).then_inc(span_found, 1)

                    def step(s, u):
                        if known(s) and LOOP_END < s <= LOOP_END + 2 * CH:
                            reach(s - LOOP_END - 1)
                        if upto_last(s + 2):
                            scale_of(s + 2, (u + 2) % UNROLL)
                        if known(s) and s == -1:
                            weights_of()
                        if upto_last(s + 3):
                            stats_of(s + 3, (u + 3) % UNROLL)
                        if known(s) and s == -2:
                            turned_weights()
                        if upto_last(s):
                            add_bias(s, u)

                    node_steps(dve, step)
                    dve.wait_ge(span_found, 2 * CH)
                    nc.vector.tensor_scalar(dmin[:], dmin[:], float(N - P), None, ALU.min).then_inc(span_chain, 1)
                    dve.wait_ge(span_chain, 1)
                    nc.vector.tensor_tensor(dspan[:], dmax[:], dmin[:], ALU.subtract).then_inc(span_chain, 1)
                    dve.wait_ge(span_turned, 1)
                    nc.vector.tensor_scalar(base_neg[:], ps_w[:, 0, 0:CH * P], -1.0, None, ALU.mult).then_inc(span_chain, 1)
                    nc.vector.tensor_copy(base_i[:], ps_w[:, 0, 0:CH * P]).then_inc(span_chain, 1)
                    nc.vector.tensor_reduce(span[:], ps_w[:, 1, 0:CH * P], AX_X, ALU.max).then_inc(span_chain, 1)
                    dve.wait_ge(span_chain, 5)
                    nc.vector.tensor_scalar(local_i[:], span[:], float(P - 1), None, ALU.is_le).then_inc(span_chain, 1)

        def group_edges(s):
            return TAIL0 if known(s) and s == LAST else s * GE

        LOOP_FROM, LOOP_TO = 3, 3 + UNROLL * ((NG - 1 - 3 - 1) // UNROLL) - 1
        STEPS_END = NG
        SEEN = LAST - 2
        assert SEEN > LOOP_TO

        def branches(eng, with_window, with_gather):
            flag = eng.value_load(local_i[0:1, 0:1], min_val=0, max_val=1)
            with eng.If(flag):
                with_window()
            with eng.Else():
                with_gather()

        def in_group(s, n):
            return (not known(s)) or 0 <= s + n < NG

        with ExitStack() as st:
            def tmp(name, shape, dt=F32):
                return st.enter_context(nc.sbuf_tensor(name, shape, dt))

            def psum(name, shape):
                return st.enter_context(nc.psum_tensor(name, shape, F32))

            def sem(name):
                return st.enter_context(nc.semaphore(name))

            edges = tmp("edges", [P, UNROLL, PER, DE])
            src_i = tmp("src_i", [P, UNROLL, PER], I32)
            dst_i = tmp("dst_i", [P, UNROLL, PER], I32)
            q_rows = tmp("q_rows", [P, UNROLL, PER, D])
            k_rows = tmp("k_rows", [P, UNROLL, PER, D])
            k_win = k_rows
            rel = tmp("rel", [P, 2, PER], BF16)
            onehot = tmp("onehot", [P, 2, PER, P])
            edgeT = tmp("edgeT", [P, 2, HALF, P])
            low = tmp("low", [P, 2, PER, P])
            mid = tmp("mid", [P, 2, PER, P])
            head = tmp("head", [P, 2, PER, H])
            head2 = tmp("head2", [P, 2, PER, H])
            ps_rel = psum("ps_rel", [P, PER, P])
            ps_z = psum("ps_z", [P, 2, PER, P])
            ps_e = psum("ps_e", [P, HALF, P])
            ps_s = psum("ps_s", [P, 2, PER, H])

            zeroed = sem("zeroed")
            edges_in = [sem(f"edges_in{u}") for u in range(UNROLL)]
            src_in = [sem(f"src_in{u}") for u in range(UNROLL)]
            dst_in = [sem(f"dst_in{u}") for u in range(UNROLL)]
            q_in = [sem(f"q_in{u}") for u in range(UNROLL)]
            k_in = [sem(f"k_in{u}") for u in range(UNROLL)]
            edge_turned = sem("edge_turned")
            edgeT_ready = sem("edgeT_ready")
            rel_ready = sem("rel_ready")
            rel_spread = sem("rel_spread")
            onehot_ready = sem("onehot_ready")
            z_ready = sem("z_ready")
            low_ready = sem("low_ready")
            mid_ready = sem("mid_ready")
            s_ready = sem("s_ready")
            score_chain = sem("score_chain")
            most_seen = sem("most_seen")

            def tile_at(b, k):
                return 2 * k + b

            with nc.Block() as block:
                @block.sync
                def _(sp):
                    LOOPS = LAST // UNROLL - 1

                    def zero(block_of_rows):
                        for r in range(COPIES):
                            sp.dma_start(acc[r][bass.ds(block_of_rows * P, P), :], zeros[:]).then_inc(zeroed, 16)

                    def load(s, u, window):
                        if not known(s) and u == 0:
                            zero((s - UNROLL) // UNROLL)
                        e0 = group_edges(s)
                        if at_least(s, UNROLL):
                            sp.wait_ge(edge_turned, s - (UNROLL - 1))
                            sp.sem_inc(passed, 1)
                        sp.dma_start(edges[:, u, :, :], edge[bass.ds(e0, GE), :].rearrange("(p j) f -> p j f", p=P)
                                     ).then_inc(edges_in[u], 16)
                        if at_least(s, UNROLL):
                            sp.wait_ge(q_in[u], count(s, u, 16 * PER, -UNROLL))
                            sp.sem_inc(passed, 1)
                        sp.dma_start(src_i[:, u, :], src[bass.ds(e0, GE)].rearrange("(p j) -> p j", p=P)
                                     ).then_inc(src_in[u], 16)
                        if at_least(s, UNROLL):
                            if window:
                                sp.wait_ge(rel_ready, s - (UNROLL - 1))
                            else:
                                sp.wait_ge(k_in[u], count(s, u, 16 * PER, -UNROLL))
                            sp.sem_inc(passed, 1)
                        sp.dma_start(dst_i[:, u, :], dst[bass.ds(e0, GE)].rearrange("(p j) -> p j", p=P)
                                     ).then_inc(dst_in[u], 16)
                        if window:
                            if at_least(s, UNROLL):
                                sp.wait_ge(z_ready, s * 2 - (2 * UNROLL - 2))
                            sp.sem_inc(passed, 1)
                            row = sp.value_load(base_i[0:1, bass.ds(s, 1)], min_val=0, max_val=N - P)
                            sp.dma_start(k_win[:, u, 0, :], k_tab[bass.ds(row, P), :]).then_inc(k_in[u], 16)

                    branches(sp, lambda: run_steps(sp, 0, UNROLL, UNROLL * (LAST // UNROLL) - 1, LAST, lambda s, u: load(s, u, True)),
                             lambda: run_steps(sp, 0, UNROLL, UNROLL * (LAST // UNROLL) - 1, LAST, lambda s, u: load(s, u, False)))
                    for rows in range(LOOPS, ROWS // P):
                        zero(rows)
                    sp.wait_ge(zeroed, 16 * COPIES * (ROWS // P))

                @block.gpsimd
                def _(pool):
                    def gather(s, u, window):
                        pool.wait_ge(src_in[u], count(s, u, 16))
                        if at_least(s, UNROLL):
                            pool.wait_ge(z_ready, s * 2 - (2 * UNROLL - 2))
                        pool.sem_inc(passed, 1)
                        for j in range(PER):
                            pool.indirect_dma_start(q_rows[:, u, j, :], None, q_tab,
                                                    bass.IndirectOffsetOnAxis(src_i[:, u, j:j + 1], 0)
                                                    ).then_inc(q_in[u], 16)
                        if not window:
                            pool.wait_ge(dst_in[u], count(s, u, 16))
                            pool.sem_inc(passed, 1)
                            for j in range(PER):
                                pool.indirect_dma_start(k_rows[:, u, j, :], None, k_tab,
                                                        bass.IndirectOffsetOnAxis(dst_i[:, u, j:j + 1], 0)
                                                        ).then_inc(k_in[u], 16)

                    branches(pool, lambda: run_steps(pool, 0, UNROLL, UNROLL * (LAST // UNROLL) - 1, LAST, lambda s, u: gather(s, u, True)),
                             lambda: run_steps(pool, 0, UNROLL, UNROLL * (LAST // UNROLL) - 1, LAST, lambda s, u: gather(s, u, False)))

                @block.tensor
                def _(pe):
                    def turn(s, u):
                        pe.wait_ge(edges_in[u], count(s, u, 16))
                        if at_least(s, 1):
                            pe.wait_ge(edgeT_ready, s)
                        for k in range(HALF):
                            last = pe.transpose(ps_e[:, k, :], edges[:, u, 2 * k:2 * k + 2, :].rearrange("p j f -> p (j f)"),
                                                ident[:])
                        last.then_inc(edge_turned, 1)

                    def spread(s, u):
                        pe.wait_ge(rel_ready, s + 1)
                        if at_least(s, 1):
                            pe.wait_ge(onehot_ready, s)
                        for b in range(2):
                            for k in range(HALF):
                                last = pe.matmul(ps_rel[:, HALF * b + k, :],
                                                 rel[:, u % 2, tile_at(b, k):tile_at(b, k) + 1].to_broadcast([P, P]),
                                                 ident_b[:], start=True, stop=True)
                        last.then_inc(rel_spread, 1)

                    def make_z(s, u, window):
                        pe.wait_ge(edgeT_ready, s + 1)
                        pe.wait_ge(k_in[u], count(s, u, 16 if window else 16 * PER))
                        if window:
                            pe.wait_ge(onehot_ready, s + 1)
                        if at_least(s, 2):
                            pe.wait_ge(mid_ready, s * 2 - 2)
                        for b in range(2):
                            bank = ps_z[:, u % 2, HALF * b:HALF * (b + 1), :]
                            lo = DE * b
                            pe.matmul(bank.rearrange("p k e -> p (k e)"), w2[lo:lo + DE, :],
                                      edgeT[lo:lo + DE, u % 2, :, :].rearrange("p k e -> p (k e)"),
                                      start=True, stop=False, skip_group_check=True)
                            if window:
                                pe.matmul(bank.rearrange("p k e -> p (k e)"), k_win[:, u, 0, :],
                                          onehot[:, u % 2, HALF * b:HALF * (b + 1), :].rearrange("p k e -> p (k e)"),
                                          start=False, stop=False, skip_group_check=True)
                            if b == 0:
                                pe.wait_ge(q_in[u], count(s, u, 16 * PER))
                            for k in range(HALF):
                                if not window:
                                    pe.matmul(ps_z[:, u % 2, HALF * b + k, :], k_rows[:, u, tile_at(b, k), :], ident[:],
                                              start=False, stop=False, skip_group_check=True)
                                last = pe.matmul(ps_z[:, u % 2, HALF * b + k, :], q_rows[:, u, tile_at(b, k), :], ident[:],
                                                 start=False, stop=(k == HALF - 1), skip_group_check=True)
                            last.then_inc(z_ready, 1)

                    def heads(s, u):
                        pe.wait_ge(mid_ready, s * 2 + 2)
                        if at_least(s, 1):
                            pe.wait_ge(score_chain, s * 3 - 2)
                        for b in range(2):
                            for k in range(HALF):
                                last = pe.matmul(ps_s[:, u % 2, tile_at(b, k), :], mid[:, u % 2, HALF * b + k, :], a2[:],
                                                 start=True, stop=True)
                        last.then_inc(s_ready, 1)

                    def step(s, u, window):
                        if in_group(s, 1):
                            turn(s + 1, (u + 1) % UNROLL)
                            if window:
                                spread(s + 1, (u + 1) % UNROLL)
                        if in_group(s, 0):
                            make_z(s, u, window)
                        if at_least(s, 1):
                            heads(s - 1, (u - 1) % UNROLL)

                    def path(window):
                        turn(0, 0)
                        if window:
                            spread(0, 0)
                        run_steps(pe, 0, LOOP_FROM, LOOP_TO, STEPS_END, lambda s, u: step(s, u, window))

                    branches(pe, lambda: path(True), lambda: path(False))

                @block.scalar
                def _(act):
                    def copy_edges(s, u):
                        act.wait_ge(edge_turned, s + 1)
                        if at_least(s, 2):
                            act.wait_ge(z_ready, s * 2 - 2)
                        nc.scalar.activation(edgeT[:, u % 2, :, :], ps_e[:], ACT.Copy).then_inc(edgeT_ready, 1)

                    def scale(s, u):
                        for b in range(2):
                            act.wait_ge(z_ready, s * 2 + (b + 1))
                            if at_least(s, 2):
                                act.wait_ge(mid_ready, s * 2 - (3 - b))
                            h0, h1 = HALF * b, HALF * (b + 1)
                            nc.scalar.activation(low[:, u % 2, h0:h1, :], ps_z[:, u % 2, h0:h1, :], ACT.Copy,
                                                 scale=SLOPE).then_inc(low_ready, 1)

                    def step(s, u):
                        if in_group(s, 1):
                            copy_edges(s + 1, (u + 1) % UNROLL)
                        if in_group(s, 0):
                            scale(s, u)

                    copy_edges(0, 0)
                    run_steps(act, 0, LOOP_FROM, LOOP_TO, LAST, step)

                @block.vector
                def _(dve):
                    def relative(s, u):
                        dve.wait_ge(dst_in[u], count(s, u, 16))
                        if at_least(s, 2):
                            dve.wait_ge(rel_spread, s - 1)
                        nc.vector.tensor_tensor(rel[:, u % 2, :], dst_i[:, u, :], base_neg[:, bass.ds(s, 1)].to_broadcast([P, PER]),
                                                ALU.add).then_inc(rel_ready, 1)

                    def one_hot(s, u):
                        dve.wait_ge(rel_spread, s + 1)
                        if at_least(s, 2):
                            dve.wait_ge(z_ready, s * 2 - 2)
                        nc.vector.tensor_scalar(onehot[:, u % 2, :, :], ps_rel[:], part[:, 0:1], None,
                                                ALU.is_equal).then_inc(onehot_ready, 1)

                    def leaky(s, u):
                        if at_least(s, 2):
                            dve.wait_ge(s_ready, s - 1)
                        for b in range(2):
                            dve.wait_ge(low_ready, s * 2 + (b + 1))
                            h0, h1 = HALF * b, HALF * (b + 1)
                            nc.vector.tensor_tensor(mid[:, u % 2, h0:h1, :], low[:, u % 2, h0:h1, :],
                                                    ps_z[:, u % 2, h0:h1, :], ALU.max).then_inc(mid_ready, 1)

                    def head_sum(s, u):
                        dve.wait_ge(s_ready, s + 1)
                        nc.vector.tensor_tensor(head[:, u % 2, :, :], ps_s[:, u % 2, :, :], b2_rep[:],
                                                ALU.add).then_inc(score_chain, 1)
                        dve.wait_ge(score_chain, s * 3 + 1)
                        nc.vector.scalar_tensor_tensor(head2[:, u % 2, :, :], head[:, u % 2, :, :], SLOPE,
                                                       head[:, u % 2, :, :], ALU.mult, ALU.max).then_inc(score_chain, 1)
                        dve.wait_ge(score_chain, s * 3 + 2)
                        nc.vector.tensor_reduce(score[:, bass.ds(s * PER, PER)], head2[:, u % 2, :, :], AX_X,
                                                ALU.add).then_inc(score_chain, 1)

                    def step(s, u, window):
                        if window:
                            if in_group(s, 2):
                                relative(s + 2, (u + 2) % UNROLL)
                            if in_group(s, 1):
                                one_hot(s + 1, (u + 1) % UNROLL)
                        if in_group(s, 0):
                            leaky(s, u)
                        if at_least(s, 1):
                            head_sum(s - 1, (u - 1) % UNROLL)
                        if known(s) and s == SEEN:
                            dve.wait_ge(score_chain, s * 3)
                            nc.vector.tensor_reduce(top_of[:, 0:1], score[:, 0:SEEN * PER], AX_X, ALU.max).then_inc(most_seen, 1)

                    def path(window):
                        if window:
                            relative(0, 0)
                            relative(1, 1)
                            one_hot(0, 0)
                        run_steps(dve, 0, LOOP_FROM, LOOP_TO, STEPS_END, lambda s, u: step(s, u, window))

                    branches(dve, lambda: path(True), lambda: path(False))

        with ExitStack() as st:
            def tmp(name, shape, dt=F32):
                return st.enter_context(nc.sbuf_tensor(name, shape, dt))

            def psum(name, shape):
                return st.enter_context(nc.psum_tensor(name, shape, F32))

            def sem(name):
                return st.enter_context(nc.semaphore(name))

            top = tmp("top", [P, 1])
            top_all = tmp("top_all", [P, 1])
            shift = tmp("shift", [P, 1])
            sums = tmp("sums", [P, 3])
            total = tmp("total", [P, 1])
            EARLY = UNROLL * PER
            NF = FULL * PER
            src_j = tmp("src_j", [P, UNROLL, PER], I32)
            dst_j = tmp("dst_j", [P, UNROLL, PER], I32)
            src_f = tmp("src_f", [P, UNROLL, PER])
            w_now = tmp("w_now", [P, UNROLL, PER])
            rel_j = tmp("rel_j", [P, 2, PER], BF16)
            one_j = tmp("one_j", [P, 2, PER, P])
            v_rows = tmp("v_rows", [P, UNROLL, PER, D])
            v_win = tmp("v_win", [P, UNROLL, D])
            w_rows = tmp("w_rows", [P, 2, PER, D])
            same = tmp("same", [P, 2, PER, P])
            same_b = tmp("same_b", [P, PER, P])
            before = tmp("before", [P, UNROLL, PER])
            dup = tmp("dup", [P, UNROLL, PER])
            move = tmp("move", [P, UNROLL, PER])
            row_i = tmp("row_i", [P, UNROLL, PER], I32)
            summed = tmp("summed", [P, UNROLL, PER, D])
            ps_r = psum("ps_r", [P, PER, P])
            ps_src = psum("ps_src", [P, PER, P])
            ps_v = psum("ps_v", [P, PER, P])
            ps_x = psum("ps_x", [P, PER, P])

            src_in = [sem(f"srcj_in{u}") for u in range(UNROLL)]
            dst_in = [sem(f"dstj_in{u}") for u in range(UNROLL)]
            v_in = [sem(f"v_in{u}") for u in range(UNROLL)]
            src_float = sem("src_float")
            w_ready = sem("w_ready")
            top_ready = sem("top_ready")
            top_spread = sem("top_spread")
            shifted = sem("shifted")
            exp_ready = sem("exp_ready")
            masked = sem("masked")
            sum_chain = sem("sum_chain")
            sum_spread = sem("sum_spread")
            rel_ready = sem("relj_ready")
            src_spread = sem("src_spread")
            counted = sem("counted")
            rel_spread = sem("relj_spread")
            one_ready = sem("onej_ready")
            same_ready = sem("same_ready")
            row_chain = sem("row_chain")
            v_made = sem("v_made")
            weighed = sem("weighed")
            x_made = sem("x_made")
            x_copied = sem("x_copied")
            added = [sem(f"added{r}") for r in range(COPIES)]
            AC = PER // COPIES
            RING_FROM = UNROLL + 1
            RING_TO = RING_FROM + UNROLL * ((NG - 2 - RING_FROM) // UNROLL) - 1

            with nc.Block() as block:
                @block.sync
                def _(sp):
                    def load(s, u, window):
                        e0 = group_edges(s)
                        if at_least(s, UNROLL):
                            sp.wait_ge(src_float, s - (UNROLL - 1))
                            sp.sem_inc(passed, 1)
                        sp.dma_start(src_j[:, u, :], src[bass.ds(e0, GE)].rearrange("(p j) -> p j", p=P)
                                     ).then_inc(src_in[u], 16)
                        if at_least(s, UNROLL):
                            if window:
                                sp.wait_ge(rel_ready, s - (UNROLL - 1))
                            else:
                                sp.wait_ge(v_in[u], count(s, u, 16 * PER, -UNROLL))
                            sp.sem_inc(passed, 1)
                        sp.dma_start(dst_j[:, u, :], dst[bass.ds(e0, GE)].rearrange("(p j) -> p j", p=P)
                                     ).then_inc(dst_in[u], 16)
                        if window:
                            if at_least(s, UNROLL):
                                sp.wait_ge(v_made, s * 2 - (2 * UNROLL - 2))
                            sp.sem_inc(passed, 1)
                            row = sp.value_load(base_i[0:1, bass.ds(s, 1)], min_val=0, max_val=N - P)
                            sp.dma_start(v_win[:, u, :], v_tab[bass.ds(row, P), :]).then_inc(v_in[u], 16)

                    branches(sp, lambda: run_steps(sp, 0, UNROLL, UNROLL * (LAST // UNROLL) - 1, LAST, lambda s, u: load(s, u, True)),
                             lambda: run_steps(sp, 0, UNROLL, UNROLL * (LAST // UNROLL) - 1, LAST, lambda s, u: load(s, u, False)))

                @block.gpsimd
                def _(pool):
                    def gather(s, u):
                        pool.wait_ge(dst_in[u], count(s, u, 16))
                        if at_least(s, UNROLL):
                            pool.wait_ge(weighed, s * 2 - (2 * UNROLL - 2))
                        pool.sem_inc(passed, 1)
                        for j in range(PER):
                            pool.indirect_dma_start(v_rows[:, u, j, :], None, v_tab,
                                                    bass.IndirectOffsetOnAxis(dst_j[:, u, j:j + 1], 0)
                                                    ).then_inc(v_in[u], 16)

                    def scatter(s, u):
                        pool.wait_ge(row_chain, s * 3 + 3)
                        for j in range(PER):
                            if j % HALF == 0:
                                pool.wait_ge(x_copied, s * 2 + (j // HALF + 1))
                            r, k = j % COPIES, j // COPIES
                            if at_least(s, 1) or k:
                                pool.wait_ge(added[r], s * (16 * AC) + 16 * k)
                            pool.sem_inc(passed, 1)
                            pool.indirect_dma_start(acc[r], bass.IndirectOffsetOnAxis(row_i[:, u, j:j + 1], 0),
                                                    summed[:, u, j, :], None, compute_op=ALU.add
                                                    ).then_inc(added[r], 16)

                    def step(s, u):
                        if in_group(s, 1):
                            gather(s + 1, (u + 1) % UNROLL)
                        if at_least(s, 1):
                            scatter(s - 1, (u - 1) % UNROLL)

                    def with_window():
                        run_steps(pool, 0, UNROLL, UNROLL * (LAST // UNROLL) - 1, LAST, scatter)

                    def with_gather():
                        gather(0, 0)
                        run_steps(pool, 0, LOOP_FROM, LOOP_TO, STEPS_END, step)

                    pool.wait_ge(top_ready, 2)
                    nc.gpsimd.partition_all_reduce(top_all[:], top[:], P, RMAX).then_inc(top_spread, 1)
                    branches(pool, with_window, with_gather)
                    pool.wait_ge(sum_chain, 2)
                    nc.gpsimd.partition_all_reduce(total_all[:], total[:], P, RADD).then_inc(sum_spread, 1)
                    for r in range(COPIES):
                        pool.wait_ge(added[r], 16 * AC * NG)

                @block.tensor
                def _(pe):
                    def spread_rel(s, u):
                        pe.wait_ge(rel_ready, s + 1)
                        for b in range(2):
                            if at_least(s, 1):
                                pe.wait_ge(one_ready, s * 2 - (1 - b))
                            for j in range(HALF * b, HALF * (b + 1)):
                                last = pe.matmul(ps_r[:, j, :], rel_j[:, u % 2, j:j + 1].to_broadcast([P, P]), ident_b[:],
                                                 start=True, stop=True)
                            last.then_inc(rel_spread, 1)

                    def spread_src(s, u):
                        pe.wait_ge(src_float, s + 1)
                        for b in range(2):
                            if at_least(s, 1):
                                pe.wait_ge(counted, s * 2 - (1 - b))
                            for j in range(HALF * b, HALF * (b + 1)):
                                last = pe.matmul(ps_src[:, j, :], src_f[:, u, j:j + 1].to_broadcast([P, P]), ident[:],
                                                 start=True, stop=True)
                            last.then_inc(src_spread, 1)

                    def values(s, u):
                        pe.wait_ge(one_ready, s * 2 + 2)
                        pe.wait_ge(v_in[u], count(s, u, 16))
                        for b in range(2):
                            if at_least(s, 1):
                                pe.wait_ge(weighed, s * 2 - (1 - b))
                            for j in range(HALF * b, HALF * (b + 1)):
                                last = pe.matmul(ps_v[:, j, :], one_j[:, u % 2, j, :], v_win[:, u, :], start=True, stop=True)
                            last.then_inc(v_made, 1)

                    def combine(s, u):
                        for b in range(2):
                            pe.wait_ge(same_ready, s * 2 + (b + 1))
                            pe.wait_ge(weighed, s * 2 + (b + 1))
                            if at_least(s, 1):
                                pe.wait_ge(x_copied, s * 2 - (1 - b))
                            for j in range(HALF * b, HALF * (b + 1)):
                                last = pe.matmul(ps_x[:, j, :], same[:, u % 2, j, :], w_rows[:, u % 2, j, :], start=True,
                                                 stop=True)
                            last.then_inc(x_made, 1)

                    def step(s, u, window):
                        if window and in_group(s, 0):
                            values(s, u)
                        if window and in_group(s, 1):
                            spread_rel(s + 1, (u + 1) % UNROLL)
                        if at_least(s, 1):
                            combine(s - 1, (u - 1) % UNROLL)
                        if in_group(s, 1):
                            spread_src(s + 1, (u + 1) % UNROLL)

                    def path(window):
                        if window:
                            spread_rel(0, 0)
                        spread_src(0, 0)
                        run_steps(pe, 0, LOOP_FROM, LOOP_TO, STEPS_END, lambda s, u: step(s, u, window))

                    branches(pe, lambda: path(True), lambda: path(False))

                @block.scalar
                def _(act):
                    def prepare(s, u, window):
                        act.wait_ge(src_in[u], count(s, u, 16))
                        if at_least(s, UNROLL):
                            act.wait_ge(row_chain, s * 3 - (3 * UNROLL - 3))
                            act.wait_ge(src_spread, s * 2 - (2 * UNROLL - 2))
                        nc.scalar.activation(src_f[:, u, :], src_j[:, u, :], ACT.Copy).then_inc(src_float, 1)
                        if window:
                            act.wait_ge(dst_in[u], count(s, u, 16))
                            if at_least(s, 2):
                                act.wait_ge(rel_spread, s * 2 - 2)
                            nc.scalar.activation(rel_j[:, u % 2, :], dst_j[:, u, :], ACT.Identity,
                                                 bias=base_neg[:, bass.ds(s, 1)]).then_inc(rel_ready, 1)

                    def weights(s, u):
                        if known(s) and s == LAST:
                            act.wait_ge(masked, 1)
                        if at_least(s, UNROLL):
                            act.wait_ge(weighed, s * 2 - (2 * UNROLL - 2))
                        nc.scalar.activation(w_now[:, u, :], weight[:, bass.ds(s * PER, PER)], ACT.Copy).then_inc(w_ready, 1)

                    def exp(part_of, lo, hi):
                        nc.scalar.activation(weight[:, lo:hi], score[:, lo:hi], ACT.Exp, bias=shift[:, 0:1], scale=1.0 / H,
                                             accum_out=sums[:, part_of:part_of + 1]).then_inc(exp_ready, 1)

                    def first_weights():
                        act.wait_ge(top_spread, 1)
                        nc.scalar.mul(shift[:], top_all[:], -1.0 / H).then_inc(shifted, 1)
                        act.wait_ge(shifted, 1)
                        exp(0, 0, EARLY)
                        act.wait_ge(exp_ready, 1)

                    def other_weights():
                        exp(1, EARLY, NF)
                        nc.scalar.activation(weight[:, NF:], score[:, NF:], ACT.Exp, bias=shift[:, 0:1],
                                             scale=1.0 / H).then_inc(exp_ready, 1)
                        act.wait_ge(exp_ready, 3)

                    def weigh(s, u, window):
                        act.wait_ge(w_ready, s + 1)
                        if not window:
                            act.wait_ge(v_in[u], count(s, u, 16 * PER))
                        for b in range(2):
                            if window:
                                act.wait_ge(v_made, s * 2 + (b + 1))
                            if at_least(s, 2):
                                act.wait_ge(x_made, s * 2 - (3 - b))
                            for j in range(HALF * b, HALF * (b + 1)):
                                op = nc.scalar.activation(w_rows[:, u % 2, j, :], ps_v[:, j, :] if window else v_rows[:, u, j, :],
                                                          ACT.Copy, scale=w_now[:, u, j:j + 1])
                            op.then_inc(weighed, 1)

                    def copy_sums(s, u):
                        for b in range(2):
                            act.wait_ge(x_made, s * 2 + (b + 1))
                            if b == 0 and at_least(s, UNROLL):
                                for r in range(COPIES):
                                    act.wait_ge(added[r], s * (16 * AC) - 16 * AC * (UNROLL - 1))
                            h0, h1 = HALF * b, HALF * (b + 1)
                            nc.scalar.activation(summed[:, u, h0:h1, :], ps_x[:, h0:h1, :], ACT.Copy).then_inc(x_copied, 1)

                    def step(s, u, window):
                        if in_group(s, 2):
                            prepare(s + 2, (u + 2) % UNROLL, window)
                            weights(s + 2, (u + 2) % UNROLL)
                        if in_group(s, 0):
                            weigh(s, u, window)
                        if at_least(s, 1):
                            copy_sums(s - 1, (u - 1) % UNROLL)
                        if known(s) and s == 1:
                            other_weights()

                    def path(window):
                        prepare(0, 0, window)
                        prepare(1, 1, window)
                        first_weights()
                        weights(0, 0)
                        weights(1, 1)
                        run_steps(act, 0, RING_FROM, RING_TO, STEPS_END, lambda s, u: step(s, u, window))

                    branches(act, lambda: path(True), lambda: path(False))

                @block.vector
                def _(dve):
                    def one_hot(s, u):
                        for b in range(2):
                            dve.wait_ge(rel_spread, s * 2 + (b + 1))
                            if b == 0 and at_least(s, 2):
                                dve.wait_ge(v_made, s * 2 - 2)
                            h0, h1 = HALF * b, HALF * (b + 1)
                            nc.vector.tensor_scalar(one_j[:, u % 2, h0:h1, :], ps_r[:, h0:h1, :], part[:, 0:1], None,
                                                    ALU.is_equal).then_inc(one_ready, 1)

                    def compare(s, u):
                        for b in range(2):
                            dve.wait_ge(src_spread, s * 2 + (b + 1))
                            if b == 0:
                                if at_least(s, 2):
                                    dve.wait_ge(x_made, s * 2 - 2)
                            h0, h1 = HALF * b, HALF * (b + 1)
                            nc.vector.tensor_tensor(same[:, u % 2, h0:h1, :], ps_src[:, h0:h1, :],
                                                    src_f[:, u, h0:h1].rearrange("p (j a) -> p j a", a=1).to_broadcast([P, HALF, P]),
                                                    ALU.is_equal).then_inc(same_ready, 1)
                            for j in range(h0, h1):
                                op = nc.vector.scalar_tensor_tensor(same_b[:, j, :], ps_src[:, j, :], src_f[:, u, j:j + 1],
                                                                    earlier[:], ALU.is_equal, ALU.mult,
                                                                    accum_out=before[:, u, j:j + 1])
                            op.then_inc(counted, 1)
                        if at_least(s, UNROLL):
                            for r in range(COPIES):
                                dve.wait_ge(added[r], s * (16 * AC) - 16 * AC * (UNROLL - 1))
                        dve.wait_ge(counted, s * 2 + 2)
                        nc.vector.tensor_scalar(dup[:, u, :], before[:, u, :], 1.0, None, ALU.min).then_inc(row_chain, 1)
                        dve.wait_ge(row_chain, s * 3 + 1)
                        nc.vector.scalar_tensor_tensor(move[:, u, :], src_f[:, u, :], part[:, 1:2], dup[:, u, :],
                                                       ALU.subtract, ALU.mult).then_inc(row_chain, 1)
                        dve.wait_ge(row_chain, s * 3 + 2)
                        nc.vector.tensor_tensor(row_i[:, u, :], src_f[:, u, :], move[:, u, :],
                                                ALU.subtract).then_inc(row_chain, 1)

                    def step(s, u, window):
                        if in_group(s, 1):
                            if window:
                                one_hot(s + 1, (u + 1) % UNROLL)
                            compare(s + 1, (u + 1) % UNROLL)
                        if known(s) and s == 2:
                            finish_weights()

                    def path(window):
                        if window:
                            one_hot(0, 0)
                        compare(0, 0)
                        run_steps(dve, 0, LOOP_FROM, LOOP_TO, LAST, lambda s, u: step(s, u, window))

                    def finish_weights():
                        dve.wait_ge(exp_ready, 3)
                        nc.vector.tensor_tensor(weight[:, NF:], weight[:, NF:], tail_mask[:], ALU.mult).then_inc(masked, 1)
                        dve.wait_ge(masked, 1)
                        nc.vector.tensor_reduce(sums[:, 2:3], weight[:, NF:], AX_X, ALU.add).then_inc(sum_chain, 1)
                        dve.wait_ge(sum_chain, 1)
                        nc.vector.tensor_reduce(total[:], sums[:], AX_X, ALU.add).then_inc(sum_chain, 1)

                    nc.vector.tensor_reduce(top_of[:, 1:2], score[:, SEEN * PER:], AX_X, ALU.max).then_inc(top_ready, 1)
                    dve.wait_ge(top_ready, 1)
                    nc.vector.tensor_reduce(top[:], top_of[:], AX_X, ALU.max).then_inc(top_ready, 1)
                    branches(dve, lambda: path(True), lambda: path(False))

        with ExitStack() as st:
            def tmp(name, shape, dt=F32):
                return st.enter_context(nc.sbuf_tensor(name, shape, dt))

            def sem(name):
                return st.enter_context(nc.semaphore(name))

            inv = tmp("inv", [P, 1])
            ident_w = tmp("ident_w", [P, P])
            sums_in = tmp("sums_in", [P, UNROLL, COPIES, NB, D])
            y_stats = tmp("y_stats", [P, UNROLL, NB, 6])
            y_mv = tmp("y_mv", [P, UNROLL, NB, 2])
            y_std = tmp("y_std", [P, UNROLL, NB])
            y_rstd = tmp("y_rstd", [P, UNROLL, NB])
            y_g = tmp("y_g", [P, UNROLL, NB, D])
            o_sb = tmp("o_sb", [P, 2, NB, D])
            ps_y = st.enter_context(nc.psum_tensor("ps_y", [P, UNROLL, NB, D], F32))

            acc_in = [sem(f"acc_in{u}") for u in range(UNROLL)]
            pair_added = sem("pair_added")
            divisor = sem("divisor")
            y_ready = sem("y_ready")
            y_chain = sem("y_chain")
            y_std_ready = sem("y_std_ready")
            y_rstd_ready = sem("y_rstd_ready")
            y_g_ready = sem("y_g_ready")
            o_ready = sem("o_ready")
            o_out = [sem("o_out0"), sem("o_out1")]

            def final_steps(eng, step):
                run_steps(eng, 0, UNROLL, NSTEP - 1, NSTEP + 1, step)

            def upto(s, n):
                return (not known(s)) or s <= n

            with nc.Block() as block:
                @block.sync
                def _(sp):
                    def load(s, u):
                        if at_least(s, UNROLL):
                            sp.wait_ge(y_ready, s - (UNROLL - 1))
                        for r in range(COPIES):
                            if known(s) and s == NSTEP:
                                sp.dma_start(sums_in[:, u, r, 0:1, :], nodes_of(acc[r], s * NB, 1)).then_inc(acc_in[u], 16)
                                sp.dma_start(sums_in[0:NREM, u, r, 1, :], nodes_of(acc[r], TR, 1)).then_inc(acc_in[u], 16)
                            else:
                                sp.dma_start(sums_in[:, u, r, :, :], nodes_of(acc[r], s * NB, NB)).then_inc(acc_in[u], 16)

                    final_steps(sp, lambda s, u: load(s, u) if upto(s, NSTEP) else None)

                @block.gpsimd
                def _(pool):
                    def step(s, u):
                        if not upto(s, NSTEP):
                            return
                        n = tiles(s)
                        if known(s) and s == NSTEP:
                            pool.wait_ge(acc_in[u], count(s, u, 16 * COPIES) + 16 * COPIES)
                        else:
                            pool.wait_ge(acc_in[u], count(s, u, 16 * COPIES))
                        a, b = (sums_in[:, u, COPIES - k, 0:n, :] for k in (2, 1))
                        nc.gpsimd.tensor_tensor(a, a, b, ALU.add).then_inc(pair_added, 1)

                    final_steps(pool, step)

                @block.tensor
                def _(pe):
                    def add_up(s, u):
                        pe.wait_ge(pair_added, s + 1)
                        if at_least(s, UNROLL):
                            pe.wait_ge(y_g_ready, (s - (UNROLL - 1)) * NB)
                        n = tiles(s)
                        y = ps_y[:, u % UNROLL, 0:n, :]
                        pe.matmul(y, ident[:], h_sb[:, bass.ds(s * NB, n), :], start=True, stop=False)
                        for r in range(COPIES - 1):
                            last = pe.matmul(y, ident_w[:], sums_in[:, u, r, 0:n, :], start=False, stop=(r == COPIES - 2))
                        last.then_inc(y_ready, 1)

                    pe.wait_ge(divisor, 2)
                    final_steps(pe, lambda s, u: add_up(s, u) if upto(s, NSTEP) else None)

                @block.scalar
                def _(act):
                    def root(s, u):
                        act.wait_ge(y_chain, (s + 1) * 2)
                        if at_least(s, UNROLL):
                            act.wait_ge(y_rstd_ready, s - (UNROLL - 1))
                        nc.scalar.activation(y_std[:, u % UNROLL, :], y_mv[:, u % UNROLL, :, 1], ACT.Sqrt, bias=eps[:, 0:1]
                                             ).then_inc(y_std_ready, 1)

                    def store(s, u):
                        act.wait_ge(o_ready, (s + 1) * NB if tiles(s) == NB else NSTEP * NB + 2)
                        if known(s) and s == NSTEP:
                            act.dma_start(nodes_of(out, s * NB, 1), o_sb[:, u % 2, 0:1, :]).then_inc(o_out[u % 2], 16)
                            act.dma_start(nodes_of(out, TR, 1), o_sb[0:NREM, u % 2, 1, :]).then_inc(o_out[u % 2], 16)
                        else:
                            act.dma_start(nodes_of(out, s * NB, NB), o_sb[:, u % 2, :, :]).then_inc(o_out[u % 2], 16)

                    def step(s, u):
                        if upto(s, NSTEP):
                            root(s, u)
                        if at_least(s, 1):
                            store(s - 1, (u - 1) % UNROLL)

                    final_steps(act, step)
                    act.wait_ge(o_out[0], 16 * (NSTEP // 2) + 32)
                    act.wait_ge(o_out[1], 16 * (NSTEP // 2))

                @block.vector
                def _(dve):
                    def measure(s, u):
                        dve.wait_ge(y_ready, s + 1)
                        n = tiles(s)
                        for k in range(n):
                            op = nc.vector.bn_stats(y_stats[:, u % UNROLL, k, :], ps_y[:, u % UNROLL, k, :])
                        op.then_inc(y_chain, 1)
                        dve.wait_ge(y_chain, s * 2 + 1)
                        if at_least(s, UNROLL):
                            dve.wait_ge(y_std_ready, s - (UNROLL - 1))
                        dve.sem_inc(passed, 1)
                        for k in range(NB):
                            op = nc.vector.bn_aggr(y_mv[:, u % UNROLL, k, :], y_stats[:, u % UNROLL, k, :])
                        op.then_inc(y_chain, 1)

                    def finish(s, u):
                        dve.wait_ge(y_std_ready, s + 1)
                        nc.vector.reciprocal(y_rstd[:, u % UNROLL, :], y_std[:, u % UNROLL, :]).then_inc(y_rstd_ready, 1)
                        n = tiles(s)
                        for k in range(n):
                            nc.vector.scalar_tensor_tensor(y_g[:, u % UNROLL, k, :], ps_y[:, u % UNROLL, k, :], y_mv[:, u % UNROLL, k, 0:1], gamma_b[:],
                                                           ALU.subtract, ALU.mult).then_inc(y_g_ready, 1)
                        dve.wait_ge(y_rstd_ready, s + 1)
                        if at_least(s, 2):
                            dve.wait_ge(o_out[u % 2], s * 8 - u % 2 * 8)
                        for k in range(n):
                            dve.wait_ge(y_g_ready, s * NB + (k + 1))
                            nc.vector.scalar_tensor_tensor(o_sb[:, u % 2, k, :], y_g[:, u % UNROLL, k, :], y_rstd[:, u % UNROLL, k:k + 1],
                                                           x_sb[:, bass.ds(s * NB + k, 1), :].rearrange("p a k -> p (a k)"),
                                                           ALU.mult, ALU.add).then_inc(o_ready, 1)

                    def step(s, u):
                        if upto(s, NSTEP):
                            measure(s, u)
                        if at_least(s, 1):
                            finish(s - 1, (u - 1) % UNROLL)

                    nc.vector.reciprocal(inv[:], total_all[:]).then_inc(divisor, 1)
                    dve.wait_ge(divisor, 1)
                    nc.vector.tensor_scalar(ident_w[:], ident[:], inv[:, 0:1], None, ALU.mult).then_inc(divisor, 1)
                    final_steps(dve, step)


NAMES = ["x", "src", "dst", "edge_attr_64"] + ["L0_gnn_" + n for n in (
    "Wn", "bn", "Wq", "bq", "Wk", "bk", "Wv", "bv", "We", "be", "A1", "b1", "A2", "b2", "gamma", "beta")]


def kernel(**inputs):
    import numpy as np
    import concourse.bacc as bacc
    from concourse.bass_utils import run_bass_kernel_spmd

    nc = bacc.Bacc("TRN2", target_bir_lowering=False, num_devices=1)
    arrays, args = {}, []
    for name in NAMES:
        a = np.ascontiguousarray(inputs[name])
        arrays[name + "_dram"] = a
        args.append(nc.dram_tensor(name + "_dram", a.shape, mybir.dt.from_np(a.dtype), kind="ExternalInput").ap())
    shape = arrays["x_dram"].shape
    args.append(nc.dram_tensor("out_dram", shape, F32, kind="ExternalOutput").ap())
    gnn_layer(nc, *args)
    r = run_bass_kernel_spmd(nc, [arrays], core_ids=[0])
    return r.results[0]["out_dram"]
```
